# Optimizing a Trainium2 kernel written in Bass

```python
import numpy as np
import jax
import jax.numpy as jnp

def _softmax(x, axis=-1):
    return jax.nn.softmax(x, axis=axis)

def _gelu(x):
    return jax.nn.gelu(x, approximate=True)

def _silu(x):
    return jax.nn.silu(x)

def _sigmoid(x):
    return jax.nn.sigmoid(x)

def _layernorm(x, axis=-1, eps=1e-05):
    m = jnp.mean(x, axis=axis, keepdims=True)
    v = jnp.var(x, axis=axis, keepdims=True)
    return (x - m) / jnp.sqrt(v + eps)

def _scatter_add(tgt, idx, src, axis=0):
    return tgt.at[idx].add(src)

def _segment_sum(src, seg, n):
    return jax.ops.segment_sum(src, seg, n)
kernel_name = 'mk_macaron_d1_jaxref_r8_d968ab'

def setup_inputs(seed: int=0):
    np.random.seed(seed)
    _w = jnp.asarray

    def _L0_attn_setup():
        import jax, jax.numpy as jnp
        import numpy as np
        D_MODEL = 128
        N_HEADS = 4
        N_KV_HEADS = 2
        HEAD_DIM = D_MODEL // N_HEADS
        N_REP = N_HEADS // N_KV_HEADS
        EPS_RMS = 1e-06
        EPS_NORM = 1e-12

        def _rmsnorm(x, w):
            var = jnp.mean(jnp.square(x), axis=-1, keepdims=True)
            return x * jax.lax.rsqrt(var + EPS_RMS) * w

        def _l2norm(x):
            n = jnp.sqrt(jnp.sum(jnp.square(x), axis=-1, keepdims=True))
            return x / jnp.maximum(n, EPS_NORM)
        key = jax.random.key(seed)
        ks = jax.random.split(key, 8)
        B, L = (2, 512)
        s = 0.02
        return {'x': jax.random.normal(ks[0], (B, L, D_MODEL), dtype=jnp.float32), 'norm_w': jnp.ones((D_MODEL,), dtype=jnp.float32), 'Wq': jax.random.normal(ks[1], (D_MODEL, N_HEADS * HEAD_DIM), dtype=jnp.float32) * s, 'Wk': jax.random.normal(ks[2], (D_MODEL, N_KV_HEADS * HEAD_DIM), dtype=jnp.float32) * s, 'Wv': jax.random.normal(ks[3], (D_MODEL, N_KV_HEADS * HEAD_DIM), dtype=jnp.float32) * s, 'Wo': jax.random.normal(ks[4], (N_HEADS * HEAD_DIM, D_MODEL), dtype=jnp.float32) * s, 'gate': jnp.asarray(0.1, dtype=jnp.float32), 'log_temperature': jnp.asarray(np.log(10.0), dtype=jnp.float32)}
    _L0_attn_in = _L0_attn_setup()

    def _L0_ffn_setup():
        import jax, jax.numpy as jnp
        import numpy as np
        DIM = 128
        HIDDEN = 384
        SCALE = 1.0 / 127.0

        def _dequant(w_int, dtype):
            return w_int.astype(dtype) * jnp.asarray(SCALE, dtype)
        key = jax.random.key(seed)
        k_x, k_g, k_u, k_d = jax.random.split(key, 4)
        x = jax.random.normal(k_x, (4, 256, DIM), dtype=jnp.float32)
        w_gate = jax.random.randint(k_g, (HIDDEN, DIM), -127, 128, dtype=jnp.int32)
        w_up = jax.random.randint(k_u, (HIDDEN, DIM), -127, 128, dtype=jnp.int32)
        w_down = jax.random.randint(k_d, (DIM, HIDDEN), -127, 128, dtype=jnp.int32)
        return {'x': x, 'w_gate': w_gate, 'w_up': w_up, 'w_down': w_down}
    _L0_ffn_in = _L0_ffn_setup()
    _d = {'L0_attn_x': _L0_attn_in['x'], 'L0_attn_norm_w': _L0_attn_in['norm_w'], 'L0_attn_Wq': _L0_attn_in['Wq'], 'L0_attn_Wk': _L0_attn_in['Wk'], 'L0_attn_Wv': _L0_attn_in['Wv'], 'L0_attn_Wo': _L0_attn_in['Wo'], 'L0_attn_gate': _L0_attn_in['gate'], 'L0_attn_log_temperature': _L0_attn_in['log_temperature'], 'L0_ffn_w_gate': _L0_ffn_in['w_gate'], 'L0_ffn_w_up': _L0_ffn_in['w_up'], 'L0_ffn_w_down': _L0_ffn_in['w_down']}
    _x0 = _d['L0_attn_x']
    _d['L0_attn_x'] = jax.random.normal(jax.random.fold_in(jax.random.key(seed), 1), (8, 1024, 128), dtype=_x0.dtype)
    del _x0
    return _d

def reference(L0_attn_x, L0_attn_norm_w, L0_attn_Wq, L0_attn_Wk, L0_attn_Wv, L0_attn_Wo, L0_attn_gate, L0_attn_log_temperature, L0_ffn_w_gate, L0_ffn_w_up, L0_ffn_w_down):

    def _L0_attn_ref(x, norm_w, Wq, Wk, Wv, Wo, gate, log_temperature):
        import jax, jax.numpy as jnp
        import numpy as np
        D_MODEL = 128
        N_HEADS = 4
        N_KV_HEADS = 2
        HEAD_DIM = D_MODEL // N_HEADS
        N_REP = N_HEADS // N_KV_HEADS
        EPS_RMS = 1e-06
        EPS_NORM = 1e-12

        def _rmsnorm(x, w):
            var = jnp.mean(jnp.square(x), axis=-1, keepdims=True)
            return x * jax.lax.rsqrt(var + EPS_RMS) * w

        def _l2norm(x):
            n = jnp.sqrt(jnp.sum(jnp.square(x), axis=-1, keepdims=True))
            return x / jnp.maximum(n, EPS_NORM)
        B, L, D = x.shape
        h = _rmsnorm(x, norm_w)
        q = (h @ Wq).reshape(B, L, N_HEADS, HEAD_DIM).transpose(0, 2, 1, 3)
        k = (h @ Wk).reshape(B, L, N_KV_HEADS, HEAD_DIM).transpose(0, 2, 1, 3)
        v = (h @ Wv).reshape(B, L, N_KV_HEADS, HEAD_DIM).transpose(0, 2, 1, 3)
        if N_REP > 1:
            k = jnp.repeat(k, N_REP, axis=1)
            v = jnp.repeat(v, N_REP, axis=1)
        q = _l2norm(q)
        k = _l2norm(k)
        scale = jnp.exp(log_temperature)
        attn = jnp.einsum('bhqd,bhkd->bhqk', q, k) * scale
        causal = jnp.tril(jnp.ones((L, L), dtype=bool))
        attn = jnp.where(causal, attn, -jnp.inf)
        attn = jax.nn.softmax(attn, axis=-1)
        out = jnp.einsum('bhqk,bhkd->bhqd', attn, v).transpose(0, 2, 1, 3).reshape(B, L, D)
        out = out @ Wo
        return x + gate * out

    def _L0_ffn_ref(x, w_gate, w_up, w_down):
        import jax, jax.numpy as jnp
        import numpy as np
        DIM = 128
        HIDDEN = 384
        SCALE = 1.0 / 127.0

        def _dequant(w_int, dtype):
            return w_int.astype(dtype) * jnp.asarray(SCALE, dtype)
        wg = _dequant(w_gate, x.dtype)
        wu = _dequant(w_up, x.dtype)
        wd = _dequant(w_down, x.dtype)
        gate = jnp.einsum('bsd,hd->bsh', x, wg)
        up = jnp.einsum('bsd,hd->bsh', x, wu)
        h = jax.nn.silu(gate) * up
        return jnp.einsum('bsh,dh->bsd', h, wd)
    x = L0_attn_x
    x = x + 0.5 * _L0_ffn_ref(_layernorm(x, axis=-1), L0_ffn_w_gate, L0_ffn_w_up, L0_ffn_w_down)
    x = x + _L0_attn_ref(_layernorm(x, axis=-1), L0_attn_norm_w, L0_attn_Wq, L0_attn_Wk, L0_attn_Wv, L0_attn_Wo, L0_attn_gate, L0_attn_log_temperature)
    x = x + 0.5 * _L0_ffn_ref(_layernorm(x, axis=-1), L0_ffn_w_gate, L0_ffn_w_up, L0_ffn_w_down)
    return x

_drawn_inputs = setup_inputs


def setup_inputs(seed=0):
    import zlib

    import numpy as np

    out = dict(_drawn_inputs(seed))
    spreads = {'L0_attn_norm_w': (1.0, 0.6)}
    factors = {'L0_attn_Wq': 64.0, 'L0_attn_Wk': 64.0, 'L0_attn_Wv': 64.0, 'L0_attn_Wo': 64.0}
    for name, (base, spread) in spreads.items():
        noise = np.random.default_rng([zlib.crc32(name.encode()), seed]).standard_normal(out[name].shape)
        drawn = base * np.exp(spread * noise) if base else spread * noise
        out[name] = jnp.asarray(drawn.astype(out[name].dtype))
    for name, factor in factors.items():
        out[name] = (out[name] * factor).astype(out[name].dtype)
    return out
```

```python
import concourse.bass as bass
from concourse import mybir
from contextlib import ExitStack

dt = mybir.dt
ALU = mybir.AluOpType
ACT = mybir.ActivationFunctionType
AXX = mybir.AxisListType.X


def macaron_kernel(nc, x, norm_w, wq, wk, wv, wo, gate, log_temp, w_gate, w_up, w_down, out):
    f32, f16, bf16, i32 = dt.float32, dt.float16, dt.bfloat16, dt.int32
    P = 128
    B, L, D = x.shape
    HID = w_gate.shape[0]
    NJ = HID // P
    DQ, DK = wq.shape[1], wk.shape[1]
    HD = 32
    NH, NKV = DQ // HD, DK // HD
    NQK = NH + NKV
    TPC = 4
    CH = TPC * P
    NT = B * L // P
    NC = NT // TPC
    TPB = L // P
    QCS = L // CH
    LN_EPS, RMS_EPS, L2_MIN = 1e-5, 1e-6, 1e-12
    QSCALE = 64.0
    MASKED = -3e38

    xt = x.rearrange("b l d -> (b l) d").rearrange("(t p) d -> p t d", p=P)
    ot = out.rearrange("b l d -> (b l) d").rearrange("(t p) d -> p t d", p=P)

    ctx = ExitStack()
    with ctx:
        def sb(name, shape, d=f32):
            return ctx.enter_context(nc.sbuf_tensor(name, shape, d))

        def sem(name):
            return ctx.enter_context(nc.semaphore(name))

        X = sb("X", [P, NT, D])
        ident16 = sb("ident16", [P, P], f16)
        ident32 = sb("ident32", [P, P])
        causal = sb("causal", [P, P], bf16)
        ones32 = sb("ones32", [P, HD])
        eps_ln = sb("eps_ln", [P, TPC])
        eps_rms = sb("eps_rms", [P, TPC])
        one = sb("one", [P, TPC])
        nhalf = sb("nhalf", [P, TPC * NQK])
        w_int = sb("w_int", [P, 3 * NJ, P], i32)
        w_flt = sb("w_flt", [P, 3 * NJ, P])
        w_nat = sb("w_nat", [P, 2, 3 * NJ, P], f16)
        WT = sb("WT", [P, 2, 3 * NJ, P], f16)
        qkvo = sb("qkvo", [P, DQ + 2 * DK + D])
        QKVO = sb("QKVO", [P, 2, DQ + 2 * DK + D], f16)
        NQKV = DQ + 2 * DK
        normw = sb("normw", [P, 1])
        colmax = sb("colmax", [P, 4])
        m4 = sb("m4", [4, 4])
        pw = sb("pw", [P, 4])
        ipw = sb("ipw", [P, 4])
        lomax = sb("lomax", [P, 1])
        lo1 = sb("lo1", [1, 1])
        loflag = sb("loflag", [1, 1], i32)
        k_silu = sb("k_silu", [P, 1])
        k_isilu = sb("k_isilu", [P, 1])
        k_ffn = sb("k_ffn", [P, 1])
        k_p2 = sb("k_p2", [P, 1])
        k_p64 = sb("k_p64", [P, 1])
        k_exp = sb("k_exp", [P, 1])
        k_wo = sb("k_wo", [P, 1])
        gate_t = sb("gate_t", [P, 1])
        lt_t = sb("lt_t", [P, 1])
        bns = sb("bns", [P, TPC, 6])
        MV = [sb(f"MV{i}", [P, TPC, 2]) for i in range(2)]
        RS = [sb(f"RS{i}", [P, TPC]) for i in range(2)]
        XN = sb("XN", [P, TPC, P])
        XS = [sb(f"XS{i}", [P, 2, TPC, P], f16) for i in range(2)]
        XT = [sb(f"XT{i}", [P, 2, CH], f16) for i in range(2)]
        SG = [sb(f"SG{i}", [P, CH]) for i in range(2)]
        H = [sb(f"H{i}", [P, CH]) for i in range(2)]
        HH = [sb(f"HH{i}", [P, NJ, CH], f16) for i in range(2)]
        HL = [sb(f"HL{i}", [P, NJ, CH], f16) for i in range(2)]
        rv = sb("rv", [P, TPC])
        RMS = sb("RMS", [P, TPC])
        A1 = sb("A1", [P, TPC])
        B1 = sb("B1", [P, TPC])
        SQ = sb("SQ", [P, TPC, NQK * HD])
        SS = sb("SS", [P, TPC, NQK])
        R = sb("R", [P, TPC, NQK])
        QN = sb("QN", [P, TPC, NQK, HD])
        ST = sb("ST", [P, TPC, NQK, 4, HD], f16)
        QT = [sb(f"QT{i}", [P, NH, L], f16) for i in range(2)]
        KT = [sb(f"KT{i}", [P, NKV, L], f16) for i in range(2)]
        V = [sb(f"V{i}", [P, TPB, DK]) for i in range(2)]
        PT = [sb(f"PT{i}", [P, NH, CH]) for i in range(2)]
        RD = sb("RD", [P, CH])
        ON = sb("ON", [P, CH])
        OH = sb("OH", [P, CH], f16)
        OL = sb("OL", [P, CH], f16)

        bank = [ctx.enter_context(nc.psum_tensor(f"bank{i}", [P, 2, CH], f32)) for i in range(4)]
        GU = bank[0:2]
        XP = bank[2][:, 0, :].bitcast(f16).rearrange("p (s n) -> p s n", s=2)
        DN = [bank[3][:, i, :].rearrange("p (t d) -> p t d", t=TPC) for i in range(2)]
        SP_ = bank[0:2]
        PV = bank[2][:, 0, :]
        DEN = bank[2][:, 1, :]
        MB = [bank[3][:, i, :] for i in range(2)]

        s_xin = [sem(f"s_xin{i}") for i in range(2)]
        (s_w, s_wo_in, s_one, s_wready, s_wprep, s_wt, s_wpe, s_kact, s_const) = [sem("s_" + n) for n in (
            "w", "wo_in", "one", "wready", "wprep", "wt", "wpe", "kact", "const")]
        (s_stat, s_rstd, s_xn, s_xh, s_xl, s_xp, s_xt, s_gu, s_silu, s_h, s_hh, s_hl, s_dn,
         s_res, s_out) = [sem("s_" + n) for n in (
            "stat", "rstd", "xn", "xh", "xl", "xp", "xt", "gu", "silu", "h", "hh", "hl", "dn",
            "res", "out")]
        (a_stat, a_rstd, a_coef, a_xn, a_y, a_xh, a_xl, a_sq, a_ss, a_r, a_hi, a_lo, a_full,
         a_free, a_s, a_exp, a_pv, a_on, a_oh, a_ol) = [sem("a_" + n) for n in (
            "stat", "rstd", "coef", "xn", "y", "xh", "xl", "sq", "ss", "r", "hi", "lo",
            "full", "free", "s", "exp", "pv", "on", "oh", "ol")]

        block = ctx.enter_context(nc.Block())

        def drive(eng, step, n, head, tail):
            for i in range(head):
                step(i, i)
            with eng.Fori(0, (n - head - tail) // 2) as it:
                for u in range(2):
                    step(head + u, it * 2 + (head + u))
            for i in range(n - tail, n):
                step(i, i)

        def tiles(c):
            return X[:, bass.ds(c * TPC, TPC), :] if not isinstance(c, int) else \
                X[:, c * TPC:(c + 1) * TPC, :]

        def tile(c, t):
            if isinstance(c, int):
                return X[:, c * TPC + t, :]
            return X[:, bass.ds(c * TPC + t, 1), :].rearrange("p t d -> p (t d)")

        def ffn_dve(e, ph):
            def stats(k, c):
                if ph == 0:
                    e.wait_ge(s_xin[k % 2], (c - k % 2) * 8 + 16)
                g = c + NC * ph
                if k >= 1 or ph:
                    e.wait_ge(s_stat, 2 * g)
                for t in range(TPC):
                    i = e.bn_stats(bns[:, t, :], tile(c, t))
                i.then_inc(s_stat, 1)

            def aggregate(k, c):
                for t in range(TPC):
                    i = e.bn_aggr(MV[k % 2][:, t, :], bns[:, t, :])
                i.then_inc(s_stat, 1)

            def normalise(k, c):
                g = c + NC * ph
                e.wait_ge(s_rstd, 2 * g + 2)
                if k >= 1 or ph:
                    e.wait_ge(s_xh, g)
                    e.wait_ge(s_xl, g)
                for t in range(TPC):
                    i = e.tensor_scalar(XN[:, t, :], tile(c, t), MV[k % 2][:, t, 0:1],
                                        RS[k % 2][:, t:t + 1], ALU.subtract, ALU.mult)
                i.then_inc(s_xn, 1)

            def xt_out(k, c):
                e.wait_ge(s_xp, c + NC * ph + 1)
                e.tensor_copy(XT[k % 2][:, :, :], XP).then_inc(s_xt, 1)

            def hidden(k, c, j):
                n = (c + NC * ph) * NJ + j
                q = (k * NJ + j) % 2
                e.wait_ge(s_silu, n + 1)
                if (k * NJ + j) >= 2 or ph:
                    e.wait_ge(s_hh, n - 1)
                    e.wait_ge(s_hl, n - 1)
                e.scalar_tensor_tensor(H[q][:, :], SG[q][:, :], k_isilu[:, 0:1], GU[q][:, 1, :],
                                       ALU.mult, ALU.mult).then_inc(s_h, 1)

            def residual(k, c):
                e.wait_ge(s_dn, c + NC * ph + 1)
                e.scalar_tensor_tensor(tiles(c), DN[k % 2], k_ffn[:, 0:1], tiles(c),
                                       ALU.mult, ALU.add).then_inc(s_res, 1)

            def step(k, c):
                if k + 1 < NC:
                    xt_out(k + 1, c + 1)
                hidden(k, c, 0)
                if k + 2 < NC:
                    stats(k + 2, c + 2)
                    e.wait_ge(s_stat, 2 * (c + 2 + NC * ph) + 1)
                hidden(k, c, 1)
                if k + 2 < NC:
                    aggregate(k + 2, c + 2)
                hidden(k, c, 2)
                if k + 2 < NC:
                    normalise(k + 2, c + 2)
                if k >= 1:
                    residual(k - 1, c - 1)

            for c in range(2):
                stats(c, c)
                e.wait_ge(s_stat, 2 * (c + NC * ph) + 1)
                aggregate(c, c)
                normalise(c, c)
                if c == 0:
                    xt_out(0, 0)
            drive(e, step, NC, 2, 2)
            residual(NC - 1, NC - 1)

        def ffn_pool(e, ph):
            def rstd(k, c):
                g = c + NC * ph
                e.wait_ge(s_stat, 2 * g + 2)
                if k >= 2 or ph:
                    e.wait_ge(s_xn, g - 1)
                e.tensor_tensor(RS[k % 2][:, :], MV[k % 2][:, :, 1], eps_ln[:, :], ALU.add)\
                    .then_inc(s_rstd, 1)
                e.wait_ge(s_rstd, 2 * g + 1)
                e.tensor_tensor(RS[k % 2][:, :], RS[k % 2][:, :], nhalf[:, 0:TPC], ALU.pow)\
                    .then_inc(s_rstd, 1)

            def x_lo(k, c):
                e.wait_ge(s_xh, c + NC * ph + 1)
                e.tensor_tensor(XS[k % 2][:, 1, :, :], XN[:, :, :], XS[k % 2][:, 0, :, :],
                                ALU.subtract).then_inc(s_xl, 1)

            def h_lo(k, c, j):
                n = (c + NC * ph) * NJ + j
                e.wait_ge(s_hh, n + 1)
                e.tensor_tensor(HL[k % 2][:, j, :], H[(k * NJ + j) % 2][:, :], HH[k % 2][:, j, :],
                                ALU.subtract).then_inc(s_hl, 1)

            def step(k, c):
                if k + 2 < NC:
                    rstd(k + 2, c + 2)
                h_lo(k, c, 0)
                h_lo(k, c, 1)
                if k + 2 < NC:
                    x_lo(k + 2, c + 2)
                h_lo(k, c, 2)

            for c in range(2):
                rstd(c, c)
                x_lo(c, c)
            drive(e, step, NC, 2, 2)

        def ffn_act(e, ph):
            def x_hi(k, c):
                g = c + NC * ph
                e.wait_ge(s_xn, g + 1)
                if k >= 2 or ph:
                    e.wait_ge(s_xp, g - 1)
                e.activation(XS[k % 2][:, 0, :, :], XN[:, :, :], ACT.Copy).then_inc(s_xh, 1)

            def silu(k, c, j):
                n = (c + NC * ph) * NJ + j
                q = (k * NJ + j) % 2
                e.wait_ge(s_gu, n + 1)
                if k * NJ + j >= 2 or ph:
                    e.wait_ge(s_h, n - 1)
                e.activation(SG[q][:, :], GU[q][:, 0, :], ACT.Silu, scale=k_silu[:, 0:1])\
                    .then_inc(s_silu, 1)

            def h_hi(k, c, j):
                n = (c + NC * ph) * NJ + j
                e.wait_ge(s_h, n + 1)
                if j == 0 and (k >= 2 or ph):
                    e.wait_ge(s_dn, c + NC * ph - 1)
                e.activation(HH[k % 2][:, j, :], H[(k * NJ + j) % 2][:, :], ACT.Copy)\
                    .then_inc(s_hh, 1)

            def step(k, c):
                silu(k, c, 0)
                silu(k, c, 1)
                h_hi(k, c, 0)
                silu(k, c, 2)
                h_hi(k, c, 1)
                if k + 2 < NC:
                    x_hi(k + 2, c + 2)
                h_hi(k, c, 2)

            for c in range(2):
                x_hi(c, c)
            drive(e, step, NC, 2, 2)

        def ffn_pe(e, ph, low):
            def x_t(k, c):
                g = c + NC * ph
                e.wait_ge(s_xl, g + 1)
                if k >= 1 or ph:
                    e.wait_ge(s_xt, g)
                for part in range(2):
                    for t in range(TPC):
                        i = e.transpose(XP[:, part, t * P:(t + 1) * P], XS[k % 2][:, part, t, :],
                                        ident16[:, :])
                i.then_inc(s_xp, 1)

            def gate_up(k, c, j):
                n = (c + NC * ph) * NJ + j
                q = (k * NJ + j) % 2
                if j == 0:
                    e.wait_ge(s_xt, c + NC * ph + 1)
                if k * NJ + j >= 2 or ph:
                    e.wait_ge(s_h, n - 1)
                for w in range(2):
                    passes = [(0, 0), (0, 1)] + [(1, 0)] * low
                    for a, (wp, xp) in enumerate(passes):
                        i = e.matmul(GU[q][:, w, :], WT[:, wp, w * NJ + j, :], XT[k % 2][:, xp, :],
                                     start=a == 0, stop=a == len(passes) - 1)
                i.then_inc(s_gu, 1)

            def down(k, c):
                g = c + NC * ph
                e.wait_ge(s_hl, (g + 1) * NJ)
                if k >= 2 or ph:
                    e.wait_ge(s_res, g - 1)
                for t in range(TPC):
                    passes = [(hp, wp, j) for hp, wp in [(0, 0), (1, 0)] + [(0, 1)] * low
                              for j in range(NJ)]
                    for a, (hp, wp, j) in enumerate(passes):
                        i = e.matmul(DN[k % 2][:, t, :],
                                     (HH, HL)[hp][k % 2][:, j, t * P:(t + 1) * P],
                                     WT[:, wp, 2 * NJ + j, :], start=a == 0,
                                     stop=a == len(passes) - 1)
                i.then_inc(s_dn, 1)

            def step(k, c):
                if k + 1 < NC:
                    x_t(k + 1, c + 1)
                for j in range(NJ):
                    gate_up(k, c, j)
                if k >= 1:
                    down(k - 1, c - 1)

            x_t(0, 0)
            drive(e, step, NC, 2, 2)
            down(NC - 1, NC - 1)

        groups = [(qc, i) for qc in range(QCS) for i in range(TPC * (qc + 1))]
        NG = len(groups)
        USES = {1: [("wo", 1)], 2: [("x", 0)], 3: [("qkv", 0, 0), ("qkv", 0, 1)],
                5: [("t", 0, 0), ("t", 0, 1)], 6: [("t", 0, 2), ("wo", 0)], 7: [("x", 1)],
                8: [("qkv", 1, 0), ("qkv", 1, 1)], 10: [("t", 1, 0), ("t", 1, 1)],
                11: [("t", 1, 2)]}
        order = [u for g in sorted(USES) for u in USES[g]]
        NU = len(order)
        assert NU % 2 == 0

        FIRST = [u for u in order if u[0] != "wo"]
        BASE = len(FIRST) - 1
        LAST = [("wo", 1), ("wo", 0)]

        def misc(b, u, k=0):
            if b is None:
                return FIRST.index(u) % 2, FIRST.index(u)
            q = (LAST if k == B - 1 else order).index(u)
            return (BASE + q) % 2, b * NU + BASE + q

        def width(g):
            qc, i = groups[g]
            return CH - max(0, i - TPC * qc) * P

        def att_pe(e):
            def scores(k, b, g, hp):
                qc, i = groups[g]
                n = width(g)
                q0 = (qc + 1) * CH - n
                G = b * NG + g
                if k * NG + g >= 1:
                    e.wait_ge(a_exp, 2 * G + hp - 1)
                diag = i >= TPC * qc
                for h in range(2):
                    o = SP_[hp][:, h, 0:n]
                    i_ = e.matmul(o, KT[k % 2][:, hp, i * P:(i + 1) * P],
                                  QT[k % 2][:, 2 * hp + h, q0:q0 + n], start=True, stop=True)
                if diag:
                    for h in range(2):
                        i_ = e.matmul(SP_[hp][:, h, 0:P], ident16[:, :], causal[:, :], start=False,
                                      stop=True, skip_group_check=True)
                i_.then_inc(a_s, 1)

            def weigh(k, b, g):
                qc, i = groups[g]
                n = width(g)
                G = b * NG + g
                e.wait_ge(a_exp, 2 * G + 2)
                if i == 0 and k * QCS + qc >= 1:
                    e.wait_ge(a_on, b * QCS + qc)
                done = i >= TPC * qc
                for h in range(NH):
                    e.matmul(PV[HD * h:HD * h + HD, CH - n:CH], V[k % 2][:, i, HD * (h // 2):
                             HD * (h // 2) + HD], PT[g % 2][:, h, 0:n], start=i == 0, stop=done,
                             skip_group_check=True)
                for h in range(NH):
                    i_ = e.matmul(DEN[HD * h:HD * h + HD, CH - n:CH], ones32[:, :],
                                  PT[g % 2][:, h, 0:n], start=i == 0, stop=done,
                                  skip_group_check=True)
                i_.then_inc(a_pv, 1)

            def use(b, q, n, u):
                if not (isinstance(n, int) and n < 2):
                    e.wait_ge(a_free, n - 1)
                if u[0] == "qkv" and u[2] == 0:
                    e.wait_ge(a_free, n)
                m16 = MB[q].bitcast(f16)
                if u[0] == "x":
                    m = b * 2 + u[1]
                    e.wait_ge(a_xl, m + 1)
                    for part in range(2):
                        for t in range(TPC):
                            i_ = e.transpose(m16[:, (part * TPC + t) * P:(part * TPC + t + 1) * P],
                                             XS[0][:, part, t, :], ident16[:, :])
                elif u[0] == "qkv":
                    for t in range(2):
                        tt = 2 * u[2] + t
                        o = MB[q][:, t * NQKV:(t + 1) * NQKV]
                        for a, (xp, wp) in enumerate([(0, 0), (1, 0), (0, 1)]):
                            i_ = e.matmul(o, XT[0][:, xp, tt * P:(tt + 1) * P],
                                          QKVO[:, wp, 0:NQKV], start=a == 0, stop=a == 2)
                elif u[0] == "t":
                    m = b * 2 + u[1]
                    e.wait_ge(a_lo, m + 1)
                    for h in range(2):
                        for t in range(TPC):
                            i_ = e.transpose(m16[:, (h * TPC + t) * P:(h * TPC + t + 1) * P],
                                             ST[:, t, 2 * u[2] + h, :, :].rearrange("p s d -> p (s d)"),
                                             ident16[:, :])
                else:
                    m = b * 2 + u[1]
                    e.wait_ge(a_ol, m + 1)
                    for t in range(TPC):
                        for a, (o_, wp) in enumerate([(OH, 0), (OL, 0), (OH, 1)]):
                            i_ = e.matmul(MB[q][:, t * P:(t + 1) * P], o_[:, t * P:(t + 1) * P],
                                          QKVO[:, wp, NQKV:], start=a == 0, stop=a == 2)
                i_.then_inc(a_full, 1)

            for u in FIRST:
                use(0, *misc(None, u), u)
            e.wait_ge(a_free, len(FIRST))
            scores(0, 0, 0, 0)
            scores(0, 0, 0, 1)

            def step(k, b):
                for g in range(NG):
                    if g + 1 < NG:
                        scores(k, b, g + 1, 0)
                        scores(k, b, g + 1, 1)
                    elif k + 1 < B:
                        scores(k + 1, b + 1, 0, 0)
                        scores(k + 1, b + 1, 0, 1)
                    weigh(k, b, g)
                    for u in USES.get(g, []):
                        if (u[0] != "wo" and k + 1 == B) or (u == ("wo", 1) and k == 0):
                            continue
                        rows_of = b + 1 if u[0] != "wo" else b - u[1]
                        use(rows_of, *misc(b, u, k), u)
            drive(e, step, B, 1, 1)
            n = B * NU + BASE - NU + len(LAST)
            use(B - 1, n % 2, n, ("wo", 1))

        def att_act(e):
            def exps(k, b, g):
                n = width(g)
                G = b * NG + g
                for hp in range(2):
                    e.wait_ge(a_s, 2 * G + hp + 1)
                    if hp == 0 and k * NG + g >= 2:
                        e.wait_ge(a_pv, G - 1)
                    e.activation(PT[g % 2][:, 2 * hp:2 * hp + 2, 0:n], SP_[hp][:, :, 0:n], ACT.Exp,
                                 scale=k_exp[:, 0:1]).then_inc(a_exp, 1)

            def x_hi(m):
                e.wait_ge(a_xn, m + 1)
                e.activation(XS[0][:, 0, :, :], XN[:, :, :], ACT.Copy).then_inc(a_xh, 1)

            def squares(kk, m, b, half):
                for c in range(2):
                    q, n = misc(b, ("qkv", half, c))
                    e.wait_ge(a_full, n + 1)
                    v = MB[q].rearrange("p (t n) -> p t n", t=2)
                    t0 = half * TPC + 2 * c
                    e.activation(V[kk % 2][:, t0:t0 + 2, :], v[:, :, DQ + DK:NQKV], ACT.Copy)
                    e.activation(SQ[:, 2 * c:2 * c + 2, :], v[:, :, 0:DQ + DK], ACT.Square)\
                        .then_inc(a_sq, 1)

            def stack_hi(b, half):
                e.wait_ge(a_free, misc(b, ("qkv", half, 1))[1] + 1)
                for t in range(TPC):
                    for s in (0, 1):
                        e.activation(ST[:, t, 0:NH, s, :], QN[:, t, 0:NH, :], ACT.Copy)
                    for s in (0, 2):
                        i = e.activation(ST[:, t, NH:NQK, s, :], QN[:, t, NH:NQK, :], ACT.Copy)
                i.then_inc(a_hi, 1)

            def o_hi(m):
                e.wait_ge(a_on, m + 1)
                e.activation(OH[:, :], ON[:, :], ACT.Copy).then_inc(a_oh, 1)

            for half in range(2):
                x_hi(half)
                squares(0, half, None, half)
                stack_hi(None, half)
            exps(0, 0, 0)

            def step(k, b):
                for g in range(NG):
                    if g + 1 < NG:
                        exps(k, b, g + 1)
                    elif k + 1 < B:
                        exps(k + 1, b + 1, 0)
                    if g == 0 and k >= 1:
                        o_hi(b * 2 - 1)
                    if g == 4:
                        o_hi(b * 2)
                    if k + 1 < B:
                        if g in (1, 5):
                            x_hi((b + 1) * 2 + (g == 5))
                        if g in (3, 8):
                            squares(k + 1, (b + 1) * 2 + (g == 8), b, int(g == 8))
                        if g in (4, 9):
                            stack_hi(b, int(g == 9))
            drive(e, step, B, 1, 1)
            o_hi(B * 2 - 1)

        def att_pool(e):
            def rstds(m, first):
                e.wait_ge(a_stat, 2 * m + 2)
                if not first:
                    e.wait_ge(a_xn, m)
                    e.wait_ge(a_y, m)
                e.tensor_tensor(rv[:, :], MV[0][:, :, 1], eps_ln[:, :], ALU.add).then_inc(a_coef, 1)
                e.wait_ge(a_coef, 5 * m + 1)
                e.tensor_tensor(RMS[:, :], rv[:, :], eps_rms[:, :], ALU.mult).then_inc(a_coef, 1)
                e.wait_ge(a_coef, 5 * m + 2)
                e.tensor_tensor(RMS[:, :], RMS[:, :], MV[0][:, :, 1], ALU.add)
                e.tensor_tensor(rv[:, :], rv[:, :], nhalf[:, 0:TPC], ALU.pow).then_inc(a_coef, 1)
                e.wait_ge(a_coef, 5 * m + 3)
                e.tensor_tensor(RMS[:, :], RMS[:, :], nhalf[:, 0:TPC], ALU.pow).then_inc(a_rstd, 1)
                e.tensor_tensor(A1[:, :], rv[:, :], one[:, :], ALU.add).then_inc(a_coef, 1)
                e.tensor_tensor(B1[:, :], rv[:, :], MV[0][:, :, 0], ALU.mult).then_inc(a_coef, 1)

            def x_lo(m):
                e.wait_ge(a_xh, m + 1)
                e.tensor_tensor(XS[0][:, 1, :, :], XN[:, :, :], XS[0][:, 0, :, :], ALU.subtract)\
                    .then_inc(a_xl, 1)

            def norms(m):
                e.wait_ge(a_ss, 2 * m + 2)
                e.tensor_tensor(R[:, :, :], SS[:, :, :],
                                nhalf[:, :].rearrange("p (t h) -> p t h", t=TPC), ALU.pow)\
                    .then_inc(a_r, 1)

            def stack_lo(m):
                e.wait_ge(a_hi, m + 1)
                for t in range(TPC):
                    e.tensor_tensor(ST[:, t, 0:NH, 2, :], QN[:, t, 0:NH, :], ST[:, t, 0:NH, 0, :],
                                    ALU.subtract)
                    i = e.tensor_tensor(ST[:, t, NH:NQK, 1, :], QN[:, t, NH:NQK, :],
                                        ST[:, t, NH:NQK, 0, :], ALU.subtract)
                i.then_inc(a_lo, 1)

            def o_lo(m):
                e.wait_ge(a_oh, m + 1)
                e.tensor_tensor(OL[:, :], ON[:, :], OH[:, :], ALU.subtract).then_inc(a_ol, 1)

            for half in range(2):
                rstds(half, half == 0)
                x_lo(half)
                norms(half)
                stack_lo(half)

            def step(k, b):
                for g in range(NG):
                    if g == 0 and k >= 1:
                        o_lo(b * 2 - 1)
                    if g == 4:
                        o_lo(b * 2)
                    if k + 1 < B:
                        m = (b + 1) * 2 + (g >= 5)
                        if g in (0, 4):
                            rstds((b + 1) * 2 + (g == 4), False)
                        if g in (1, 5):
                            x_lo(m)
                        if g in (3, 8):
                            norms(m)
                        if g in (4, 9):
                            stack_lo((b + 1) * 2 + (g == 9))
            drive(e, step, B, 1, 1)
            o_lo(B * 2 - 1)

        def att_dve(e):
            def stats(m, c, first=False):
                if not first:
                    e.wait_ge(a_coef, 5 * m)
                    e.wait_ge(a_stat, 2 * m)
                for t in range(TPC):
                    i = e.bn_stats(bns[:, t, :], tile(c, t))
                i.then_inc(a_stat, 1)

            def aggregate(m):
                for t in range(TPC):
                    i = e.bn_aggr(MV[0][:, t, :], bns[:, t, :])
                i.then_inc(a_stat, 1)

            def normalise(m, c, first=False):
                e.wait_ge(a_rstd, m + 1)
                if not first:
                    e.wait_ge(a_xl, m)
                for t in range(TPC):
                    i = e.tensor_scalar(XN[:, t, :], tile(c, t), MV[0][:, t, 0:1],
                                        RMS[:, t:t + 1], ALU.subtract, ALU.mult)
                i.then_inc(a_xn, 1)
                e.wait_ge(a_coef, 5 * m + 5)
                e.wait_ge(a_xn, m + 1)
                for t in range(TPC):
                    i = e.tensor_scalar(tile(c, t), tile(c, t), A1[:, t:t + 1], B1[:, t:t + 1],
                                        ALU.mult, ALU.subtract)
                i.then_inc(a_y, 1)

            def xt_out(b, half):
                q, n = misc(b, ("x", half))
                e.wait_ge(a_full, n + 1)
                e.tensor_copy(XT[0][:, :, :], MB[q].bitcast(f16).rearrange("p (s n) -> p s n", s=2))\
                    .then_inc(a_free, 1)

            def sums(m):
                for c in range(1):
                    e.wait_ge(a_sq, 2 * m + 2)
                e.tensor_reduce(SS[:, :, :], SQ[:, :, :].rearrange("p t (h d) -> p t h d", d=HD),
                                AXX, ALU.add).then_inc(a_ss, 1)
                e.wait_ge(a_ss, 2 * m + 1)
                e.tensor_scalar(SS[:, :, :], SS[:, :, :], k_p2[:, 0:1], L2_MIN * L2_MIN,
                                ALU.mult, ALU.max).then_inc(a_ss, 1)

            def unit(m, b, half):
                e.wait_ge(a_r, m + 1)
                e.tensor_scalar(R[:, :, :], R[:, :, :], k_p64[:, 0:1], None, ALU.mult)\
                    .then_inc(a_s2, 1)
                e.wait_ge(a_s2, m + 1)
                for c in range(2):
                    q, n = misc(b, ("qkv", half, c))
                    v = MB[q].rearrange("p (t n) -> p t n", t=2)
                    i = e.tensor_tensor(
                        QN[:, 2 * c:2 * c + 2, :, :],
                        v[:, :, 0:DQ + DK].rearrange("p t (h d) -> p t h d", d=HD),
                        R[:, 2 * c:2 * c + 2, :].unsqueeze(3).to_broadcast([P, 2, NQK, HD]),
                        ALU.mult)
                    i.then_inc(a_free, 1)

            def t_out(kk, b, half, j):
                q, n = misc(b, ("t", half, j))
                e.wait_ge(a_full, n + 1)
                src = MB[q].bitcast(f16).rearrange("p (h n) -> p h n", h=2)
                cols = slice(half * CH, half * CH + CH)
                dst = QT[kk % 2][:, 2 * j:2 * j + 2, cols] if j < 2 else KT[kk % 2][:, :, cols]
                e.tensor_copy(dst, src).then_inc(a_free, 1)

            def o_norm(m, G, first=False):
                e.wait_ge(a_pv, G)
                e.reciprocal(RD[:, :], DEN).then_inc(a_rd, 1)
                e.wait_ge(a_rd, m + 1)
                if not first:
                    e.wait_ge(a_ol, m)
                e.tensor_tensor(ON[:, :], PV, RD[:, :], ALU.mult).then_inc(a_on, 1)

            def wo_out(n_q, n, c):
                e.wait_ge(a_full, n + 1)
                e.scalar_tensor_tensor(
                    tiles(c), MB[n_q].rearrange("p (t d) -> p t d", t=TPC), k_wo[:, 0:1], tiles(c),
                    ALU.mult, ALU.add).then_inc(a_free, 1)

            for half in range(2):
                stats(half, half, half == 0)
                e.wait_ge(a_stat, 2 * half + 1)
                aggregate(half)
                normalise(half, half, half == 0)
                xt_out(None, half)
                sums(half)
                unit(half, None, half)
                for j in range(3):
                    t_out(0, None, half, j)

            def step(k, b):
                m0 = (b + 1) * 2
                nxt = k + 1 < B
                for g in range(NG):
                    if g in (0, 3) and nxt:
                        stats(m0 + (g == 3), m0 + (g == 3))
                        e.wait_ge(a_stat, 2 * (m0 + (g == 3)) + 1)
                    if g == 0 and k >= 1:
                        o_norm(b * 2 - 1, b * NG)
                    if g == 4:
                        o_norm(b * 2, b * NG + TPC, k == 0)
                    if g == 0 and nxt:
                        aggregate(m0)
                        normalise(m0, m0)
                    if g == 1:
                        if k >= 1:
                            wo_out(*misc(b, ("wo", 1), k), b * 2 - 1)
                    if nxt:
                        if g in (2, 7):
                            xt_out(b, int(g == 7))
                        if g in (3, 8):
                            sums(m0 + (g == 8))
                        if g in (4, 9):
                            if g == 4:
                                aggregate(m0 + 1)
                            unit(m0 + (g == 9), b, int(g == 9))
                            if g == 4:
                                normalise(m0 + 1, m0 + 1)
                        if g in (5, 10):
                            t_out(k + 1, b, int(g == 10), 0)
                            t_out(k + 1, b, int(g == 10), 1)
                        if g in (6, 11):
                            t_out(k + 1, b, int(g == 11), 2)
                    if g == 6:
                        wo_out(*misc(b, ("wo", 0), k), b * 2)
            drive(e, step, B, 1, 1)
            o_norm(B * 2 - 1, B * NG)
            n = B * NU + BASE - NU + len(LAST)
            wo_out(n % 2, n, B * 2 - 1)
        a_s2 = sem("a_s2")
        a_rd = sem("a_rd")

        def at(v):
            return [[0, P], [1, 1]]

        @block.sync
        def _(e):
            e.dma_start(X[:, 0:TPC, :], xt[:, 0:TPC, :]).then_inc(s_xin[0], 16)
            e.dma_start(w_int[:, 0:NJ, :], w_gate.rearrange("(j p) d -> p j d", p=P)).then_inc(s_w, 16)
            e.dma_start(w_int[:, NJ:2 * NJ, :], w_up.rearrange("(j p) d -> p j d", p=P))\
                .then_inc(s_w, 16)
            e.dma_start(w_int[:, 2 * NJ:3 * NJ, :], w_down.rearrange("d (j p) -> d j p", p=P))\
                .then_inc(s_w, 16)
            e.dma_start(X[:, TPC:2 * TPC, :], xt[:, TPC:2 * TPC, :]).then_inc(s_xin[1], 16)
            for c in range(2, NC):
                e.wait_ge(s_xin[c % 2], (c // 2) * 16)
                e.dma_start(X[:, c * TPC:(c + 1) * TPC, :], xt[:, c * TPC:(c + 1) * TPC, :])\
                    .then_inc(s_xin[c % 2], 16)
            for c in range(NC):
                e.wait_ge(s_res, NC + c + 1)
                e.dma_start(ot[:, c * TPC:(c + 1) * TPC, :], X[:, c * TPC:(c + 1) * TPC, :])\
                    .then_inc(s_out, 16)
            e.wait_ge(s_out, NC * 16)

        @block.gpsimd
        def _(e):
            e.memset(ident16[:, :], 0.0)
            e.memset(ident32[:, :], 0.0)
            e.memset(causal[:, :], 0.0)
            e.memset(ones32[:, :], 1.0)
            e.memset(nhalf[:, :], -0.5)
            e.memset(eps_ln[:, :], LN_EPS)
            e.memset(eps_rms[:, :], RMS_EPS)
            e.memset(one[:, :], 1.0)
            e.memset(ST[:, :, :, 3, :], 0.0).then_inc(s_const, 1)
            e.wait_ge(s_const, 1)
            e.memset(ST[:, :, NH:NQK, 3, 0:1], 1.0)
            for m in (ident16, ident32):
                e.affine_select(out=m[:, :], in_=m[:, :], compare_op=ALU.not_equal, fill=1.0, base=0,
                                pattern=[[-1, P]], channel_multiplier=1)
            e.affine_select(out=causal[:, :], in_=causal[:, :], compare_op=ALU.is_ge, fill=MASKED,
                            base=0, pattern=[[1, P]], channel_multiplier=-1).then_inc(s_const, 1)
            ffn_pool(e, 0)
            att_pool(e)
            ffn_pool(e, 1)

        @block.scalar
        def _(e):
            e.dma_start(qkvo[:, 0:DQ], wq).then_inc(s_wo_in, 16)
            e.dma_start(qkvo[:, DQ:DQ + DK], wk).then_inc(s_wo_in, 16)
            e.dma_start(qkvo[:, DQ + DK:NQKV], wv).then_inc(s_wo_in, 16)
            e.dma_start(qkvo[:, NQKV:], wo).then_inc(s_wo_in, 16)
            e.dma_start(normw[:, :], norm_w.rearrange("(p a) -> p a", a=1)).then_inc(s_wo_in, 16)
            e.dma_start(gate_t[:, :], bass.AP(gate.tensor, 0, at(0))).then_inc(s_wo_in, 16)
            e.dma_start(lt_t[:, :], bass.AP(log_temp.tensor, 0, at(0))).then_inc(s_wo_in, 16)
            e.wait_ge(s_wo_in, 7 * 16)
            e.activation(k_exp[:, :], lt_t[:, :], ACT.Exp).then_inc(s_kact, 1)
            e.wait_ge(s_wready, 1)
            ffn_act(e, 0)
            att_act(e)
            ffn_act(e, 1)

        @block.vector
        def _(e):
            n = [0]

            def link(i):
                n[0] += 1
                i.then_inc(s_one, 1)
                e.wait_ge(s_one, n[0])

            e.wait_ge(s_w, 3 * 16)
            link(e.tensor_copy(w_flt[:, :, :], w_int[:, :, :]))
            e.tensor_reduce(colmax[:, 0:1], w_flt[:, 0:2 * NJ, :].rearrange("p a b -> p (a b)"), AXX,
                            ALU.max, apply_absolute_value=True)
            e.tensor_reduce(colmax[:, 1:2], w_flt[:, 2 * NJ:, :].rearrange("p a b -> p (a b)"), AXX,
                            ALU.max, apply_absolute_value=True)
            e.wait_ge(s_wo_in, 7 * 16)
            link(e.tensor_scalar(qkvo[:, 0:NQKV], qkvo[:, 0:NQKV], normw[:, 0:1], None, ALU.mult))
            e.tensor_reduce(colmax[:, 2:3], qkvo[:, 0:NQKV], AXX, ALU.max, apply_absolute_value=True)
            e.tensor_reduce(colmax[:, 3:4], qkvo[:, NQKV:], AXX, ALU.max, apply_absolute_value=True)\
                .then_inc(s_wprep, 1)
            e.wait_ge(s_wpe, 1)
            link(e.tensor_reduce(m4[:, 0:1], bank[0][0:4, 0, 0:P], AXX, ALU.max))
            link(e.tensor_scalar(m4[:, 1:2], m4[:, 0:1], 1e-30, None, ALU.max))
            link(e.tensor_scalar(m4[:, 2:3].bitcast(i32), m4[:, 1:2].bitcast(i32), 0x7f800000, None,
                                 ALU.bitwise_and))
            e.tensor_scalar(m4[:, 3:4], m4[:, 2:3], 2.0, None, ALU.mult).then_inc(s_wprep, 1)
            e.wait_ge(s_wpe, 2)
            link(e.tensor_copy(pw[:, :], bank[1][:, 0, 0:4]))
            link(e.tensor_scalar(ipw[:, :].bitcast(i32), pw[:, :].bitcast(i32), -1.0,
                                 float(0x7f000000), ALU.mult, ALU.add))
            link(e.tensor_scalar(w_flt[:, 0:2 * NJ, :], w_flt[:, 0:2 * NJ, :], ipw[:, 0:1], None,
                                 ALU.mult))
            link(e.tensor_scalar(w_flt[:, 2 * NJ:, :], w_flt[:, 2 * NJ:, :], ipw[:, 1:2], None,
                                 ALU.mult))
            link(e.tensor_copy(w_nat[:, 0, :, :], w_flt[:, :, :]))
            link(e.tensor_tensor(w_nat[:, 1, :, :], w_flt[:, :, :], w_nat[:, 0, :, :], ALU.subtract))
            e.tensor_reduce(lomax[:, :], w_nat[:, 1, :, :].rearrange("p a b -> p (a b)"), AXX,
                            ALU.max, apply_absolute_value=True).then_inc(s_wprep, 1)
            e.wait_ge(s_wpe, 3)
            link(e.tensor_reduce(lo1[:, :], bank[1][0:1, 1, 0:P], AXX, ALU.max))
            e.tensor_scalar(loflag[:, :], lo1[:, :], 0.0, None, ALU.is_gt).then_inc(s_wprep, 1)
            w16 = WT[:, :, :, :].rearrange("p s j n -> p (s j) n")
            for r in range(3):
                e.wait_ge(s_wpe, 4 + r)
                lo, hi = 8 * r, min(8 * r + 8, 6 * NJ)
                src = bank[2 + r // 2][:, r % 2, :].bitcast(f16).rearrange("p (j n) -> p j n", n=P)
                e.tensor_copy(w16[:, lo:hi, :], src[:, 0:hi - lo, :])
            link(e.tensor_scalar(qkvo[:, 0:NQKV], qkvo[:, 0:NQKV], ipw[:, 2:3], None, ALU.mult))
            link(e.tensor_scalar(qkvo[:, NQKV:], qkvo[:, NQKV:], ipw[:, 3:4], None, ALU.mult))
            link(e.tensor_copy(QKVO[:, 0, :], qkvo[:, :]))
            link(e.tensor_tensor(QKVO[:, 1, :], qkvo[:, :], QKVO[:, 0, :], ALU.subtract))
            link(e.tensor_scalar(k_silu[:, :], pw[:, 0:1], 1.0 / 127.0, None, ALU.mult))
            link(e.reciprocal(k_isilu[:, :], k_silu[:, :]))
            link(e.tensor_scalar(k_ffn[:, :], k_silu[:, :], k_silu[:, 0:1], 0.5 / 127.0, ALU.mult,
                                 ALU.mult))
            link(e.tensor_scalar(k_ffn[:, :], k_ffn[:, :], pw[:, 1:2], None, ALU.mult))
            link(e.tensor_scalar(k_p2[:, :], pw[:, 2:3], pw[:, 2:3], None, ALU.mult))
            link(e.tensor_scalar(k_p64[:, :], pw[:, 2:3], QSCALE, None, ALU.mult))
            link(e.tensor_scalar(k_wo[:, :], gate_t[:, :], pw[:, 2:3], pw[:, 3:4], ALU.mult, ALU.mult))
            e.wait_ge(s_kact, 1)
            e.tensor_scalar(k_exp[:, :], k_exp[:, :], 1.0 / (QSCALE * QSCALE), None, ALU.mult)\
                .then_inc(s_wready, 1)
            e.wait_ge(s_const, 2)
            ffn_dve(e, 0)
            att_dve(e)
            ffn_dve(e, 1)

        @block.tensor
        def _(e):
            e.wait_ge(s_const, 2)
            e.wait_ge(s_wprep, 1)
            e.matmul(bank[0][0:4, 0, 0:P], colmax[:, :], ident32[:, :], is_transpose=True,
                     start=True, stop=True).then_inc(s_wpe, 1)
            e.wait_ge(s_wprep, 2)
            e.matmul(bank[1][:, 0, 0:4], m4[:, 3:4].to_broadcast([4, P]), ident32[0:4, 0:4],
                     start=True, stop=True).then_inc(s_wpe, 1)
            e.wait_ge(s_wprep, 3)
            e.matmul(bank[1][0:1, 1, 0:P], lomax[:, :], ident32[:, :], is_transpose=True,
                     start=True, stop=True).then_inc(s_wpe, 1)
            blocks = [(s, j) for s in range(2) for j in range(3 * NJ)]
            for r in range(3):
                dst = bank[2 + r // 2][:, r % 2, :].bitcast(f16)
                for a, (s, j) in enumerate(blocks[8 * r:8 * r + 8]):
                    i = e.transpose(dst[:, a * P:(a + 1) * P], w_nat[:, s, j, :], ident16[:, :])
                i.then_inc(s_wpe, 1)
            e.wait_ge(s_wready, 1)
            low = e.value_load(loflag[0:1, 0:1], min_val=0, max_val=1)

            def ffn(ph):
                with e.If(low > 0):
                    ffn_pe(e, ph, 1)
                with e.Else():
                    ffn_pe(e, ph, 0)
            ffn(0)
            e.wait_ge(s_res, NC)
            att_pe(e)
            e.wait_ge(a_free, B * NU + BASE - NU + len(LAST) + 1)
            ffn(1)


_INS = ["L0_attn_x", "L0_attn_norm_w", "L0_attn_Wq", "L0_attn_Wk", "L0_attn_Wv", "L0_attn_Wo",
        "L0_attn_gate", "L0_attn_log_temperature", "L0_ffn_w_gate", "L0_ffn_w_up", "L0_ffn_w_down"]


def kernel(**inputs):
    import numpy as _np
    import concourse.bacc as _bacc
    from concourse.bass_utils import run_bass_kernel_spmd as _run

    nc = _bacc.Bacc("TRN2", target_bir_lowering=False, num_devices=1)
    arrays, args = {}, []
    for name in _INS:
        a = _np.ascontiguousarray(inputs[name])
        if a.ndim == 0:
            a = a.reshape(1)
        arrays[f"in_{name}"] = a
        args.append(nc.dram_tensor(f"in_{name}", a.shape, mybir.dt.from_np(a.dtype),
                                   kind="ExternalInput").ap())
    shape = arrays["in_L0_attn_x"].shape
    args.append(nc.dram_tensor("result", shape, mybir.dt.float32, kind="ExternalOutput").ap())
    macaron_kernel(nc, *args)
    r = _run(nc, [arrays], core_ids=[0])
    return r.results[0]["result"]
```

```python
import concourse.bass as bass
from concourse import mybir
from contextlib import ExitStack

dt = mybir.dt
ALU = mybir.AluOpType
ACT = mybir.ActivationFunctionType
AXX = mybir.AxisListType.X


def macaron_kernel(nc, x, norm_w, wq, wk, wv, wo, gate, log_temp, w_gate, w_up, w_down, out):
    f32, f16, bf16, i32 = dt.float32, dt.float16, dt.bfloat16, dt.int32
    P = 128
    B, L, D = x.shape
    HID = w_gate.shape[0]
    NJ = HID // P
    DQ, DK = wq.shape[1], wk.shape[1]
    HD = 32
    NH, NKV = DQ // HD, DK // HD
    NQK = NH + NKV
    TPC = 4
    CH = TPC * P
    NT = B * L // P
    NC = NT // TPC
    TPB = L // P
    QCS = L // CH
    LN_EPS, RMS_EPS, L2_MIN = 1e-5, 1e-6, 1e-12
    QSCALE = 64.0
    MASKED = -3e38

    xt = x.rearrange("b l d -> (b l) d").rearrange("(t p) d -> p t d", p=P)
    ot = out.rearrange("b l d -> (b l) d").rearrange("(t p) d -> p t d", p=P)

    ctx = ExitStack()
    with ctx:
        def sb(name, shape, d=f32):
            return ctx.enter_context(nc.sbuf_tensor(name, shape, d))

        def sem(name):
            return ctx.enter_context(nc.semaphore(name))

        X = sb("X", [P, NT, D])
        ident16 = sb("ident16", [P, P], f16)
        ident32 = sb("ident32", [P, P])
        causal = sb("causal", [P, P], bf16)
        ones32 = sb("ones32", [P, HD])
        eps_ln = sb("eps_ln", [P, TPC])
        eps_rms = sb("eps_rms", [P, TPC])
        one = sb("one", [P, TPC])
        nhalf = sb("nhalf", [P, TPC * NQK])
        w_int = sb("w_int", [P, 3 * NJ, P], i32)
        w_flt = sb("w_flt", [P, 3 * NJ, P])
        w_nat = sb("w_nat", [P, 2, 3 * NJ, P], f16)
        WT = sb("WT", [P, 2, 3 * NJ, P], f16)
        qkvo = sb("qkvo", [P, DQ + 2 * DK + D])
        QKVO = sb("QKVO", [P, 2, DQ + 2 * DK + D], f16)
        NQKV = DQ + 2 * DK
        normw = sb("normw", [P, 1])
        colmax = sb("colmax", [P, 4])
        m4 = sb("m4", [4, 4])
        pw = sb("pw", [P, 4])
        ipw = sb("ipw", [P, 4])
        lomax = sb("lomax", [P, 1])
        lo1 = sb("lo1", [1, 1])
        loflag = sb("loflag", [1, 1], i32)
        k_silu = sb("k_silu", [P, 1])
        k_isilu = sb("k_isilu", [P, 1])
        k_ffn = sb("k_ffn", [P, 1])
        k_lim = sb("k_lim", [P, 1])
        k_exp = sb("k_exp", [P, 1])
        k_wo = sb("k_wo", [P, 1])
        gate_t = sb("gate_t", [P, 1])
        lt_t = sb("lt_t", [P, 1])
        bns = sb("bns", [P, TPC, 6])
        MV = [sb(f"MV{i}", [P, TPC, 2]) for i in range(2)]
        RS = [sb(f"RS{i}", [P, TPC]) for i in range(2)]
        XN = [sb(f"XN{i}", [P, TPC, P]) for i in range(2)]
        XS = [sb(f"XS{i}", [P, 2, TPC, P], f16) for i in range(2)]
        XT = [sb(f"XT{i}", [P, 2, CH], f16) for i in range(2)]
        SG = [sb(f"SG{i}", [P, CH]) for i in range(NJ)]
        H = [sb(f"H{i}", [P, CH]) for i in range(NJ)]
        HH = [sb(f"HH{i}", [P, NJ, CH], f16) for i in range(2)]
        HL = [sb(f"HL{i}", [P, NJ, CH], f16) for i in range(2)]
        rv = sb("rv", [P, TPC])
        RMS = sb("RMS", [P, TPC])
        A1 = sb("A1", [P, TPC])
        B1 = sb("B1", [P, TPC])
        SQ = sb("SQ", [P, TPC, NQK * HD])
        SS = [sb(f"SS{i}", [P, TPC, NQK]) for i in range(2)]
        R = [sb(f"R{i}", [P, TPC, NQK]) for i in range(2)]
        QN = sb("QN", [P, TPC, NQK, HD])
        ST = sb("ST", [P, TPC, NQK, 4, HD], f16)
        QT = [sb(f"QT{i}", [P, NH, L], f16) for i in range(2)]
        KT = [sb(f"KT{i}", [P, NKV, L], f16) for i in range(2)]
        V = [sb(f"V{i}", [P, TPB, NQKV]) for i in range(2)]
        PT = [sb(f"PT{i}", [P, NH, CH]) for i in range(2)]
        PVS = sb("PVS", [P, 2, CH])
        RD = sb("RD", [P, CH])
        bridge = sb("bridge", [P, 1])
        ON = sb("ON", [P, CH])
        OH = sb("OH", [P, CH], f16)
        OL = sb("OL", [P, CH], f16)

        bank = [ctx.enter_context(nc.psum_tensor(f"bank{i}", [P, 2, CH], f32)) for i in range(4)]
        GU = bank[0:2]
        XP = bank[2][:, 0, :].bitcast(f16).rearrange("p (s n) -> p s n", s=2)
        DN = [bank[3][:, i, :].rearrange("p (t d) -> p t d", t=TPC) for i in range(2)]
        SP_ = bank[0:2]
        PVD = bank[2][:, :, :]
        MB = [bank[3][:, i, :] for i in range(2)]

        s_xl = [sem(f"s_xl{i}") for i in range(2)]
        s_xin = [sem(f"s_xin{i}") for i in range(2)]
        (s_w, s_wo_in, s_one, s_wready, s_wprep, s_wt, s_wpe, s_kact, s_const) = [sem("s_" + n) for n in (
            "w", "wo_in", "one", "wready", "wprep", "wt", "wpe", "kact", "const")]
        (s_stat, s_rstd, s_xn, s_xh, s_xp, s_xt, s_gu, s_silu, s_h, s_hh, s_hl, s_dn,
         s_res, s_out) = [sem("s_" + n) for n in (
            "stat", "rstd", "xn", "xh", "xp", "xt", "gu", "silu", "h", "hh", "hl", "dn",
            "res", "out")]
        (a_stat, a_rstd, a_coef, a_xn, a_y, a_xh, a_xl, a_sq, a_ss, a_r, a_qn, a_hi, a_h2, a_lo, a_full,
         a_free, a_cp, a_s, a_exp, a_pv, a_pvc, a_rd, a_on, a_oh, a_ol) = [sem("a_" + n) for n in (
            "stat", "rstd", "coef", "xn", "y", "xh", "xl", "sq", "ss", "r", "qn", "hi", "h2", "lo",
            "full", "free", "cp", "s", "exp", "pv", "pvc", "rd", "on", "oh", "ol")]

        block = ctx.enter_context(nc.Block())

        def drive(eng, step, n, head, tail):
            for i in range(head):
                step(i, i)
            with eng.Fori(0, (n - head - tail) // 2) as it:
                for u in range(2):
                    step(head + u, it * 2 + (head + u))
            for i in range(n - tail, n):
                step(i, i)

        def tiles(c):
            return X[:, bass.ds(c * TPC, TPC), :] if not isinstance(c, int) else \
                X[:, c * TPC:(c + 1) * TPC, :]

        def tile(c, t):
            if isinstance(c, int):
                return X[:, c * TPC + t, :]
            return X[:, bass.ds(c * TPC + t, 1), :].rearrange("p t d -> p (t d)")

        def ffn_x_lo(e, k, c, ph):
            e.wait_ge(s_xh, c + NC * ph + 1)
            e.tensor_tensor(XS[k % 2][:, 1, :, :], XN[k % 2][:, :, :], XS[k % 2][:, 0, :, :],
                            ALU.subtract).then_inc(s_xl[k % 2], 2)

        def ffn_dve(e, ph):
            def stats(k, c):
                if ph == 0:
                    e.wait_ge(s_xin[k % 2], (c - k % 2) * 8 + 16)
                g = c + NC * ph
                if k >= 1 or ph:
                    e.wait_ge(s_stat, 2 * g)
                for t in range(TPC):
                    i = e.bn_stats(bns[:, t, :], tile(c, t))
                i.then_inc(s_stat, 1)

            def aggregate(k, c):
                for t in range(TPC):
                    i = e.bn_aggr(MV[k % 2][:, t, :], bns[:, t, :])
                i.then_inc(s_stat, 1)

            def normalise(k, c):
                g = c + NC * ph
                e.wait_ge(s_rstd, 2 * g + 2)
                if k >= 2 or ph:
                    e.wait_ge(s_xl[k % 2], g - k % 2)
                for t in range(TPC):
                    i = e.tensor_scalar(XN[k % 2][:, t, :], tile(c, t), MV[k % 2][:, t, 0:1],
                                        RS[k % 2][:, t:t + 1], ALU.subtract, ALU.mult)
                i.then_inc(s_xn, 1)

            def hidden(k, c, j):
                n = (c + NC * ph) * NJ + j
                q = (k * NJ + j) % 2
                e.wait_ge(s_silu, n + 1)
                if k >= 1 or ph:
                    e.wait_ge(s_hh, n - NJ + 1)
                    e.wait_ge(s_hl, n - NJ + 1)
                e.scalar_tensor_tensor(H[j][:, :], SG[j][:, :], k_isilu[:, 0:1], GU[q][:, 1, :],
                                       ALU.mult, ALU.mult).then_inc(s_h, 1)

            def residual(k, c):
                e.wait_ge(s_dn, c + NC * ph + 1)
                e.scalar_tensor_tensor(tiles(c), DN[k % 2], k_ffn[:, 0:1], tiles(c),
                                       ALU.mult, ALU.add).then_inc(s_res, 1)

            def step(k, c):
                if k + 3 < NC:
                    e.wait_ge(s_stat, 2 * (c + 3 + NC * ph) + 1)
                if k + 2 < NC:
                    normalise(k + 2, c + 2)
                if k + 3 < NC:
                    aggregate(k + 3, c + 3)
                hidden(k, c, 0)
                hidden(k, c, 1)
                if k + 2 < NC and k % 2:
                    ffn_x_lo(e, k + 2, c + 2, ph)
                if k >= 2:
                    residual(k - 2, c - 2)
                hidden(k, c, 2)
                if k + 4 < NC:
                    stats(k + 4, c + 4)

            for c in range(4):
                stats(c, c)
                if c < 3:
                    e.wait_ge(s_stat, 2 * (c + NC * ph) + 1)
                    aggregate(c, c)
                if c < 2:
                    normalise(c, c)
                if c == 1:
                    ffn_x_lo(e, c, c, ph)
            drive(e, step, NC, 4, 4)
            residual(NC - 2, NC - 2)
            residual(NC - 1, NC - 1)

        def ffn_pool(e, ph):
            def rstd(k, c):
                g = c + NC * ph
                e.wait_ge(s_stat, 2 * g + 2)
                if k >= 2 or ph:
                    e.wait_ge(s_xn, g - 1)
                e.tensor_tensor(RS[k % 2][:, :], MV[k % 2][:, :, 1], eps_ln[:, :], ALU.add)\
                    .then_inc(s_rstd, 1)
                e.wait_ge(s_rstd, 2 * g + 1)
                e.tensor_tensor(RS[k % 2][:, :], RS[k % 2][:, :], nhalf[:, 0:TPC], ALU.pow)\
                    .then_inc(s_rstd, 1)

            def h_lo(k, c, j):
                n = (c + NC * ph) * NJ + j
                e.wait_ge(s_hh, n + 1)
                e.tensor_tensor(HL[k % 2][:, j, :], H[j][:, :], HH[k % 2][:, j, :],
                                ALU.subtract).then_inc(s_hl, 1)

            def step(k, c):
                if k >= 1:
                    h_lo(k - 1, c - 1, 1)
                    h_lo(k - 1, c - 1, 2)
                if k + 2 < NC and not k % 2:
                    ffn_x_lo(e, k + 2, c + 2, ph)
                if k + 3 < NC:
                    rstd(k + 3, c + 3)
                h_lo(k, c, 0)

            for c in range(3):
                rstd(c, c)
                if c == 0:
                    ffn_x_lo(e, c, c, ph)
            drive(e, step, NC, 4, 4)
            h_lo(NC - 1, NC - 1, 1)
            h_lo(NC - 1, NC - 1, 2)

        def ffn_act(e, ph):
            def x_hi(k, c):
                g = c + NC * ph
                e.wait_ge(s_xn, g + 1)
                if k >= 2 or ph:
                    e.wait_ge(s_xp, g - 1)
                e.activation(XS[k % 2][:, 0, :, :], XN[k % 2][:, :, :], ACT.Copy).then_inc(s_xh, 1)

            def xt_out(k, c):
                e.wait_ge(s_xp, c + NC * ph + 1)
                e.activation(XT[k % 2][:, :, :], XP, ACT.Copy).then_inc(s_xt, 1)

            def silu(k, c, j):
                n = (c + NC * ph) * NJ + j
                q = (k * NJ + j) % 2
                e.wait_ge(s_gu, n + 1)
                if k >= 1 or ph:
                    e.wait_ge(s_h, n - NJ + 1)
                e.activation(SG[j][:, :], GU[q][:, 0, :], ACT.Silu, scale=k_silu[:, 0:1])\
                    .then_inc(s_silu, 1)

            def h_hi(k, c, j):
                n = (c + NC * ph) * NJ + j
                e.wait_ge(s_h, n + 1)
                if j == 0 and (k >= 2 or ph):
                    e.wait_ge(s_dn, c + NC * ph - 1)
                e.activation(HH[k % 2][:, j, :], H[j][:, :], ACT.Copy)\
                    .then_inc(s_hh, 1)

            def step(k, c):
                if k >= 1:
                    h_hi(k - 1, c - 1, 2)
                silu(k, c, 0)
                if k + 2 < NC:
                    x_hi(k + 2, c + 2)
                silu(k, c, 1)
                h_hi(k, c, 0)
                silu(k, c, 2)
                if k + 1 < NC:
                    xt_out(k + 1, c + 1)
                h_hi(k, c, 1)

            for c in range(2):
                x_hi(c, c)
            xt_out(0, 0)
            drive(e, step, NC, 4, 4)
            h_hi(NC - 1, NC - 1, 2)

        def ffn_pe(e, ph, low):
            def x_t(k, c):
                g = c + NC * ph
                e.wait_ge(s_xl[k % 2], g - k % 2 + 2)
                if k >= 1 or ph:
                    e.wait_ge(s_xt, g)
                for part in range(2):
                    for t in range(TPC):
                        i = e.transpose(XP[:, part, t * P:(t + 1) * P], XS[k % 2][:, part, t, :],
                                        ident16[:, :])
                i.then_inc(s_xp, 1)

            def gate_up(k, c, j):
                n = (c + NC * ph) * NJ + j
                q = (k * NJ + j) % 2
                if j == 0:
                    e.wait_ge(s_xt, c + NC * ph + 1)
                if k * NJ + j >= 2 or ph:
                    e.wait_ge(s_h, n - 1)
                for w in range(2):
                    passes = [(0, 0), (0, 1)] + [(1, 0)] * low
                    for a, (wp, xp) in enumerate(passes):
                        i = e.matmul(GU[q][:, w, :], WT[:, wp, w * NJ + j, :], XT[k % 2][:, xp, :],
                                     start=a == 0, stop=a == len(passes) - 1)
                i.then_inc(s_gu, 1)

            def down(k, c):
                g = c + NC * ph
                e.wait_ge(s_hl, (g + 1) * NJ)
                if k >= 2 or ph:
                    e.wait_ge(s_res, g - 1)
                for t in range(TPC):
                    passes = [(hp, wp, j) for hp, wp in [(0, 0), (1, 0)] + [(0, 1)] * low
                              for j in range(NJ)]
                    for a, (hp, wp, j) in enumerate(passes):
                        i = e.matmul(DN[k % 2][:, t, :],
                                     (HH, HL)[hp][k % 2][:, j, t * P:(t + 1) * P],
                                     WT[:, wp, 2 * NJ + j, :], start=a == 0,
                                     stop=a == len(passes) - 1)
                i.then_inc(s_dn, 1)

            def step(k, c):
                for j in range(NJ):
                    gate_up(k, c, j)
                    if j == 1 and k + 1 < NC:
                        x_t(k + 1, c + 1)
                if k >= 1:
                    down(k - 1, c - 1)

            x_t(0, 0)
            drive(e, step, NC, 4, 4)
            down(NC - 1, NC - 1)

        groups = [(qc, i) for qc in range(QCS) for i in range(TPC * (qc + 1))]
        NG = len(groups)
        G0 = TPC

        USES = {2: [("x", 0)], 3: [("qkv", 0, 0), ("qkv", 0, 1), ("x", 1)],
                4: [("qkv", 1, 0), ("qkv", 1, 1)], 5: [("wo", 1)],
                7: [("t", 0, 0), ("t", 0, 1)], 8: [("t", 0, 2), ("wo", 0)],
                10: [("t", 1, 0), ("t", 1, 1)], 11: [("t", 1, 2)]}
        FIRST = [("x", 0), ("qkv", 0, 0), ("qkv", 0, 1), ("x", 1), ("qkv", 1, 0), ("qkv", 1, 1)] + \
                [("t", h, j) for h in range(2) for j in range(3)]

        def uses_in(k, g):
            return [u for u in USES.get(g, [])
                    if not (u[0] != "wo" and k == B - 1) and not (u == ("wo", 1) and k == 0)]

        seq = [(None, u) for u in FIRST] + [(k, u) for k in range(B) for g in range(NG)
                                            for u in uses_in(k, g)] + [(B, ("wo", 1))]
        reads = {a_cp: 0, a_free: 0}
        USE = {}
        for n, (k, u) in enumerate(seq):
            s = a_cp if u[0] == "qkv" else a_free
            reads[s] += 1
            USE[k, u] = (n, s, reads[s])
        PER = {a_cp: 4, a_free: 10, a_full: 14}

        def at_batch(s, k, b, v):
            return v if k is None or isinstance(b, int) else v + (b - k) * PER[s]

        def await_full(e, k, b, u):
            n = USE[k, u][0]
            e.wait_ge(a_full, at_batch(a_full, k, b, n + 1))
            return MB[n % 2]

        def await_read(e, k, b, u):
            n, s, v = USE[k, u]
            e.wait_ge(s, at_batch(s, k, b, v))

        def width(g):
            qc, i = groups[g]
            return CH - max(0, i - TPC * qc) * P

        def att_pe(e):
            def scores(k, b, g, hp):
                qc, i = groups[g]
                n = width(g)
                q0 = (qc + 1) * CH - n
                G = b * NG + g
                if k * NG + g >= 1:
                    e.wait_ge(a_exp, 2 * G + hp - 1)
                if hp == 0 and i == 0:
                    u = ("t", qc, 2)
                    await_read(e, *((k - 1, b - 1) if k else (None, None)), u)
                diag = i >= TPC * qc
                for h in range(2):
                    o = SP_[hp][:, h, 0:n]
                    i_ = e.matmul(o, KT[k % 2][:, hp, i * P:(i + 1) * P],
                                  QT[k % 2][:, 2 * hp + h, q0:q0 + n], start=True, stop=True)
                if diag:
                    for h in range(2):
                        i_ = e.matmul(SP_[hp][:, h, 0:P], ident16[:, :], causal[:, :], start=False,
                                      stop=True, skip_group_check=True)
                i_.then_inc(a_s, 1)

            def weigh(k, b, g):
                qc, i = groups[g]
                n = width(g)
                G = b * NG + g
                e.wait_ge(a_exp, 2 * G + 2)
                if i == 0 and k * QCS + qc >= 1:
                    e.wait_ge(a_pvc, b * QCS + qc)
                done = i >= TPC * qc
                for h in range(NH):
                    v0 = DQ + DK + HD * (h // 2)
                    e.matmul(PVD[HD * h:HD * h + HD, 0, CH - n:CH], V[k % 2][:, i, v0:v0 + HD],
                             PT[g % 2][:, h, 0:n], start=i == 0, stop=done, skip_group_check=True)
                for h in range(NH):
                    i_ = e.matmul(PVD[HD * h:HD * h + HD, 1, CH - n:CH], ones32[:, :],
                                  PT[g % 2][:, h, 0:n], start=i == 0, stop=done,
                                  skip_group_check=True)
                i_.then_inc(a_pv, 1)

            def use(k, b, u):
                rb = 0 if k is None else b + 1 if u[0] != "wo" else b - u[1]
                n = USE[k, u][0]
                q = n % 2
                if n >= 2:
                    pk, pu = seq[n - 2]
                    if k is None or isinstance(b, int):
                        await_read(e, pk, pk, pu)
                    else:
                        await_read(e, pk, b + (pk - k), pu)
                m16 = MB[q].bitcast(f16)
                if u[0] == "x":
                    half = u[1]
                    e.wait_ge(a_xl, rb * 2 + half + 1)
                    for part in range(2):
                        for t in range(TPC):
                            i_ = e.transpose(m16[:, (part * TPC + t) * P:(part * TPC + t + 1) * P],
                                             XS[half][:, part, t, :], ident16[:, :])
                elif u[0] == "qkv":
                    half = u[1]
                    await_read(e, k, b, ("x", half))
                    for t in range(2):
                        tt = 2 * u[2] + t
                        for a, (xp, wp) in enumerate([(0, 0), (1, 0), (0, 1)]):
                            i_ = e.matmul(MB[q][:, t * NQKV:(t + 1) * NQKV],
                                          XT[half][:, xp, tt * P:(tt + 1) * P],
                                          QKVO[:, wp, 0:NQKV], start=a == 0, stop=a == 2)
                elif u[0] == "t":
                    e.wait_ge(a_lo, rb * 2 + u[1] + 1)
                    e.wait_ge(a_h2, rb * 2 + u[1] + 1)
                    for h in range(2):
                        for t in range(TPC):
                            i_ = e.transpose(
                                m16[:, (h * TPC + t) * P:(h * TPC + t + 1) * P],
                                ST[:, t, 2 * u[2] + h, :, :].rearrange("p s d -> p (s d)"),
                                ident16[:, :])
                else:
                    e.wait_ge(a_ol, rb * 2 + u[1] + 1)
                    for t in range(TPC):
                        for a, (o_, wp) in enumerate([(OH, 0), (OL, 0), (OH, 1)]):
                            i_ = e.matmul(MB[q][:, t * P:(t + 1) * P], o_[:, t * P:(t + 1) * P],
                                          QKVO[:, wp, NQKV:], start=a == 0, stop=a == 2)
                i_.then_inc(a_full, 1)

            for u in FIRST:
                use(None, None, u)
            scores(0, 0, 0, 0)
            scores(0, 0, 0, 1)

            def step(k, b):
                for g in range(NG):
                    if g + 1 < NG:
                        scores(k, b, g + 1, 0)
                        scores(k, b, g + 1, 1)
                    elif k + 1 < B:
                        scores(k + 1, b + 1, 0, 0)
                        scores(k + 1, b + 1, 0, 1)
                    weigh(k, b, g)
                    for u in uses_in(k, g):
                        use(k, b, u)
            drive(e, step, B, 1, 1)
            use(B, B, ("wo", 1))

        def att_act(e):
            def exps(k, b, g):
                n = width(g)
                G = b * NG + g
                for hp in range(2):
                    e.wait_ge(a_s, 2 * G + hp + 1)
                    if hp == 0 and k * NG + g >= 2:
                        e.wait_ge(a_pv, G - 1)
                    e.activation(PT[g % 2][:, 2 * hp:2 * hp + 2, 0:n], SP_[hp][:, :, 0:n], ACT.Exp,
                                 scale=k_exp[:, 0:1]).then_inc(a_exp, 1)

            def x_hi(m, half):
                e.wait_ge(a_xn, m + 1)
                e.activation(XS[half][:, 0, :, :], XN[half][:, :, :], ACT.Copy).then_inc(a_xh, 1)

            def qkv_out(kk, m, k, b, half):
                for c in range(2):
                    src = await_full(e, k, b, ("qkv", half, c))
                    t0 = half * TPC + 2 * c
                    e.activation(V[kk % 2][:, t0:t0 + 2, :], src.rearrange("p (t n) -> p t n", t=2),
                                 ACT.Copy).then_inc(a_cp, 1)
                await_read(e, k, b, ("qkv", half, 1))
                t0 = half * TPC
                if not (isinstance(m, int) and m < 1):
                    e.wait_ge(a_ss, 2 * m - 1)
                e.activation(SQ[:, :, :], V[kk % 2][:, t0:t0 + TPC, 0:DQ + DK], ACT.Square)\
                    .then_inc(a_sq, 1)

            def stack_hi(m):
                e.wait_ge(a_qn, m + 1)
                e.activation(ST[:, :, :, 0, :], QN[:, :, :, :], ACT.Copy).then_inc(a_hi, 1)

            def o_hi(m):
                e.wait_ge(a_on, m + 1)
                e.activation(OH[:, :], ON[:, :], ACT.Copy).then_inc(a_oh, 1)

            def pv_out(m, G, first=False):
                e.wait_ge(a_pv, G)
                if not first:
                    e.wait_ge(a_on, m)
                e.activation(PVS[:, :, :], PVD, ACT.Copy).then_inc(a_pvc, 1)

            for half in range(2):
                x_hi(half, half)
            for half in range(2):
                qkv_out(0, half, None, None, half)
            for half in range(2):
                stack_hi(half)
            exps(0, 0, 0)

            def step(k, b):
                m0 = 2 * (b + 1)
                for g in range(NG):
                    if g == 0 and k >= 1:
                        pv_out(b * 2 - 1, b * NG)
                    if g == G0:
                        pv_out(b * 2, b * NG + G0, k == 0)
                    if g + 1 < NG:
                        exps(k, b, g + 1)
                    elif k + 1 < B:
                        exps(k + 1, b + 1, 0)
                    if g == 4 and k >= 1:
                        o_hi(b * 2 - 1)
                    if g == 7:
                        o_hi(b * 2)
                    if k + 1 < B:
                        if g in (1, 2):
                            x_hi(m0 + g - 1, g - 1)
                        if g in (3, 5):
                            qkv_out(k + 1, m0 + (g == 5), k, b, int(g == 5))
                        if g in (6, 8):
                            stack_hi(m0 + (g == 8))
            drive(e, step, B, 1, 1)
            pv_out(B * 2 - 1, B * NG)
            o_hi(B * 2 - 1)

        def att_pool(e):
            def rstds(m, first):
                e.wait_ge(a_stat, 2 * m + 2)
                if not first:
                    e.wait_ge(a_xn, m)
                    e.wait_ge(a_y, m)
                e.tensor_tensor(rv[:, :], MV[0][:, :, 1], eps_ln[:, :], ALU.add).then_inc(a_coef, 1)
                e.wait_ge(a_coef, 5 * m + 1)
                e.tensor_tensor(RMS[:, :], rv[:, :], eps_rms[:, :], ALU.mult).then_inc(a_coef, 1)
                e.wait_ge(a_coef, 5 * m + 2)
                e.tensor_tensor(RMS[:, :], RMS[:, :], MV[0][:, :, 1], ALU.add)
                e.tensor_tensor(rv[:, :], rv[:, :], nhalf[:, 0:TPC], ALU.pow).then_inc(a_coef, 1)
                e.wait_ge(a_coef, 5 * m + 3)
                e.tensor_tensor(RMS[:, :], RMS[:, :], nhalf[:, 0:TPC], ALU.pow).then_inc(a_rstd, 1)
                e.tensor_tensor(A1[:, :], rv[:, :], one[:, :], ALU.add).then_inc(a_coef, 1)
                e.tensor_tensor(B1[:, :], rv[:, :], MV[0][:, :, 0], ALU.mult).then_inc(a_coef, 1)

            def x_lo(m, half):
                e.wait_ge(a_xh, m + 1)
                e.tensor_tensor(XS[half][:, 1, :, :], XN[half][:, :, :], XS[half][:, 0, :, :],
                                ALU.subtract).then_inc(a_xl, 1)

            def norms(m, half):
                e.wait_ge(a_ss, 2 * m + 2)
                if not (isinstance(m, int) and m < 2):
                    e.wait_ge(a_qn, m - 1)
                e.tensor_tensor(R[half][:, :, :], SS[half][:, :, :],
                                nhalf[:, :].rearrange("p (t h) -> p t h", t=TPC), ALU.pow)\
                    .then_inc(a_r, 1)

            def stack_lo(m):
                e.wait_ge(a_hi, m + 1)
                e.tensor_tensor(ST[:, :, 0:NH, 2, :], QN[:, :, 0:NH, :], ST[:, :, 0:NH, 0, :],
                                ALU.subtract)
                e.tensor_tensor(ST[:, :, NH:NQK, 1, :], QN[:, :, NH:NQK, :],
                                ST[:, :, NH:NQK, 0, :], ALU.subtract).then_inc(a_lo, 1)

            def o_lo(m):
                e.wait_ge(a_oh, m + 1)
                e.tensor_tensor(OL[:, :], ON[:, :], OH[:, :], ALU.subtract).then_inc(a_ol, 1)

            for half in range(2):
                rstds(half, half == 0)
                x_lo(half, half)
            norms(0, 0)
            norms(1, 1)
            stack_lo(0)
            stack_lo(1)

            def step(k, b):
                m0 = 2 * (b + 1)
                nxt = k + 1 < B
                if nxt:
                    rstds(m0, False)
                    x_lo(m0, 0)
                    rstds(m0 + 1, False)
                    x_lo(m0 + 1, 1)
                if k >= 1:
                    o_lo(b * 2 - 1)
                if nxt:
                    norms(m0, 0)
                    norms(m0 + 1, 1)
                    stack_lo(m0)
                o_lo(b * 2)
                if nxt:
                    stack_lo(m0 + 1)
            drive(e, step, B, 1, 1)
            o_lo(B * 2 - 1)

        def att_dve(e):
            def stats(m, c, first=False):
                if not first:
                    e.wait_ge(a_coef, 5 * m)
                    e.wait_ge(a_stat, 2 * m)
                for t in range(TPC):
                    i = e.bn_stats(bns[:, t, :], tile(c, t))
                i.then_inc(a_stat, 1)
                e.wait_ge(a_stat, 2 * m + 1)
                e.memset(bridge[:, :], 0.0)
                for t in range(TPC):
                    i = e.bn_aggr(MV[0][:, t, :], bns[:, t, :])
                i.then_inc(a_stat, 1)

            def normalise(m, c, half):
                e.wait_ge(a_rstd, m + 1)
                if not (isinstance(m, int) and m < 2):
                    e.wait_ge(a_xl, m - 1)
                for t in range(TPC):
                    i = e.tensor_scalar(XN[half][:, t, :], tile(c, t), MV[0][:, t, 0:1],
                                        RMS[:, t:t + 1], ALU.subtract, ALU.mult)
                i.then_inc(a_xn, 1)

            def add_norm(m, c):
                e.wait_ge(a_coef, 5 * m + 5)
                e.wait_ge(a_xn, m + 1)
                for t in range(TPC):
                    i = e.tensor_scalar(tile(c, t), tile(c, t), A1[:, t:t + 1], B1[:, t:t + 1],
                                        ALU.mult, ALU.subtract)
                i.then_inc(a_y, 1)

            def xt_out(k, b, half):
                src = await_full(e, k, b, ("x", half))
                e.tensor_copy(XT[half][:, :, :], src.bitcast(f16).rearrange("p (s n) -> p s n", s=2))\
                    .then_inc(a_free, 1)

            def sums(m, half):
                e.wait_ge(a_sq, m + 1)
                if not (isinstance(m, int) and m < 2):
                    e.wait_ge(a_r, m - 1)
                e.tensor_reduce(SS[half][:, :, :], SQ[:, :, :].rearrange("p t (h d) -> p t h d", d=HD),
                                AXX, ALU.add).then_inc(a_ss, 1)
                e.wait_ge(a_ss, 2 * m + 1)
                e.tensor_scalar(SS[half][:, :, :], SS[half][:, :, :], 1.0 / (QSCALE * QSCALE), k_lim[:, 0:1],
                                ALU.mult, ALU.max).then_inc(a_ss, 1)

            def unit(kk, m, half):
                e.wait_ge(a_r, m + 1)
                e.wait_ge(a_lo, m)
                t0 = half * TPC
                e.tensor_tensor(
                    QN[:, :, :, :],
                    V[kk % 2][:, t0:t0 + TPC, 0:DQ + DK].rearrange("p t (h d) -> p t h d", d=HD),
                    R[half][:, :, :].unsqueeze(3).to_broadcast([P, TPC, NQK, HD]), ALU.mult)\
                    .then_inc(a_qn, 1)

            def stack_hi2(m):
                e.wait_ge(a_hi, m + 1)
                e.tensor_copy(ST[:, :, 0:NH, 1, :], ST[:, :, 0:NH, 0, :])
                e.tensor_copy(ST[:, :, NH:NQK, 2, :], ST[:, :, NH:NQK, 0, :]).then_inc(a_h2, 1)

            def t_out(kk, k, b, half, j):
                src = await_full(e, k, b, ("t", half, j)).bitcast(f16)
                src = src.rearrange("p (h n) -> p h n", h=2)
                cols = slice(half * CH, half * CH + CH)
                dst = QT[kk % 2][:, 2 * j:2 * j + 2, cols] if j < 2 else KT[kk % 2][:, :, cols]
                e.tensor_copy(dst, src).then_inc(a_free, 1)

            def o_norm(m, first=False):
                e.wait_ge(a_pvc, m + 1)
                if not first:
                    e.wait_ge(a_ol, m)
                e.reciprocal(RD[:, :], PVS[:, 1, :]).then_inc(a_rd, 1)
                e.wait_ge(a_rd, m + 1)
                e.tensor_tensor(ON[:, :], PVS[:, 0, :], RD[:, :], ALU.mult).then_inc(a_on, 1)

            def wo_out(k, b, u, c):
                src = await_full(e, k, b, u).rearrange("p (t d) -> p t d", t=TPC)
                e.scalar_tensor_tensor(tiles(c), src, k_wo[:, 0:1], tiles(c), ALU.mult, ALU.add)\
                    .then_inc(a_free, 1)

            for half in range(2):
                stats(half, half, half == 0)
                normalise(half, half, half)
                add_norm(half, half)
                xt_out(None, None, half)
            sums(0, 0)
            sums(1, 1)
            for half in range(2):
                unit(0, half, half)
                stack_hi2(half)
                for j in range(3):
                    t_out(0, None, None, half, j)

            def step(k, b):
                m0 = (b + 1) * 2
                nxt = k + 1 < B
                if nxt:
                    stats(m0, m0)
                    normalise(m0, m0, 0)
                    add_norm(m0, m0)
                    stats(m0 + 1, m0 + 1)
                    normalise(m0 + 1, m0 + 1, 1)
                    xt_out(k, b, 0)
                    add_norm(m0 + 1, m0 + 1)
                    xt_out(k, b, 1)
                if k >= 1:
                    o_norm(b * 2 - 1)
                if nxt:
                    sums(m0, 0)
                    sums(m0 + 1, 1)
                if k >= 1:
                    wo_out(k, b, ("wo", 1), b * 2 - 1)
                if nxt:
                    unit(k + 1, m0, 0)
                    stack_hi2(m0)
                o_norm(b * 2, k == 0)
                if nxt:
                    for j in range(3):
                        t_out(k + 1, k, b, 0, j)
                    unit(k + 1, m0 + 1, 1)
                    stack_hi2(m0 + 1)
                wo_out(k, b, ("wo", 0), b * 2)
                if nxt:
                    for j in range(3):
                        t_out(k + 1, k, b, 1, j)
            drive(e, step, B, 1, 1)
            o_norm(B * 2 - 1)
            wo_out(B, B, ("wo", 1), B * 2 - 1)

        def at(v):
            return [[0, P], [1, 1]]

        @block.sync
        def _(e):
            e.dma_start(X[:, 0:TPC, :], xt[:, 0:TPC, :]).then_inc(s_xin[0], 16)
            e.dma_start(w_int[:, 0:NJ, :], w_gate.rearrange("(j p) d -> p j d", p=P)).then_inc(s_w, 16)
            e.dma_start(w_int[:, NJ:2 * NJ, :], w_up.rearrange("(j p) d -> p j d", p=P))\
                .then_inc(s_w, 16)
            e.dma_start(w_int[:, 2 * NJ:3 * NJ, :], w_down.rearrange("d (j p) -> d j p", p=P))\
                .then_inc(s_w, 16)
            e.dma_start(X[:, TPC:2 * TPC, :], xt[:, TPC:2 * TPC, :]).then_inc(s_xin[1], 16)
            for c in range(2, NC):
                e.wait_ge(s_xin[c % 2], (c // 2) * 16)
                e.dma_start(X[:, c * TPC:(c + 1) * TPC, :], xt[:, c * TPC:(c + 1) * TPC, :])\
                    .then_inc(s_xin[c % 2], 16)
            for c in range(NC):
                e.wait_ge(s_res, NC + c + 1)
                e.dma_start(ot[:, c * TPC:(c + 1) * TPC, :], X[:, c * TPC:(c + 1) * TPC, :])\
                    .then_inc(s_out, 16)
            e.wait_ge(s_out, NC * 16)

        @block.gpsimd
        def _(e):
            e.memset(ident16[:, :], 0.0)
            e.memset(ident32[:, :], 0.0)
            e.memset(causal[:, :], 0.0)
            e.memset(ones32[:, :], 1.0)
            e.memset(nhalf[:, :], -0.5)
            e.memset(eps_ln[:, :], LN_EPS)
            e.memset(eps_rms[:, :], RMS_EPS)
            e.memset(one[:, :], 1.0)
            e.memset(ST[:, :, :, 3, :], 0.0).then_inc(s_const, 1)
            e.wait_ge(s_const, 1)
            e.memset(ST[:, :, NH:NQK, 3, 0:1], 1.0)
            for m in (ident16, ident32):
                e.affine_select(out=m[:, :], in_=m[:, :], compare_op=ALU.not_equal, fill=1.0, base=0,
                                pattern=[[-1, P]], channel_multiplier=1)
            e.affine_select(out=causal[:, :], in_=causal[:, :], compare_op=ALU.is_ge, fill=MASKED,
                            base=0, pattern=[[1, P]], channel_multiplier=-1).then_inc(s_const, 1)
            ffn_pool(e, 0)
            att_pool(e)
            ffn_pool(e, 1)

        @block.scalar
        def _(e):
            e.dma_start(qkvo[:, 0:DQ], wq).then_inc(s_wo_in, 16)
            e.dma_start(qkvo[:, DQ:DQ + DK], wk).then_inc(s_wo_in, 16)
            e.dma_start(qkvo[:, DQ + DK:NQKV], wv).then_inc(s_wo_in, 16)
            e.dma_start(qkvo[:, NQKV:], wo).then_inc(s_wo_in, 16)
            e.dma_start(normw[:, :], norm_w.rearrange("(p a) -> p a", a=1)).then_inc(s_wo_in, 16)
            e.dma_start(gate_t[:, :], bass.AP(gate.tensor, 0, at(0))).then_inc(s_wo_in, 16)
            e.dma_start(lt_t[:, :], bass.AP(log_temp.tensor, 0, at(0))).then_inc(s_wo_in, 16)
            e.wait_ge(s_wo_in, 7 * 16)
            e.activation(k_exp[:, :], lt_t[:, :], ACT.Exp).then_inc(s_kact, 1)
            e.wait_ge(s_wready, 1)
            ffn_act(e, 0)
            att_act(e)
            ffn_act(e, 1)

        @block.vector
        def _(e):
            n = [0]

            def link(i):
                n[0] += 1
                i.then_inc(s_one, 1)
                e.wait_ge(s_one, n[0])

            e.wait_ge(s_w, 3 * 16)
            link(e.tensor_copy(w_flt[:, :, :], w_int[:, :, :]))
            e.tensor_reduce(colmax[:, 0:1], w_flt[:, 0:2 * NJ, :].rearrange("p a b -> p (a b)"), AXX,
                            ALU.max, apply_absolute_value=True)
            e.tensor_reduce(colmax[:, 1:2], w_flt[:, 2 * NJ:, :].rearrange("p a b -> p (a b)"), AXX,
                            ALU.max, apply_absolute_value=True)
            e.wait_ge(s_wo_in, 7 * 16)
            link(e.tensor_scalar(qkvo[:, 0:NQKV], qkvo[:, 0:NQKV], normw[:, 0:1], None, ALU.mult))
            e.tensor_reduce(colmax[:, 2:3], qkvo[:, 0:NQKV], AXX, ALU.max, apply_absolute_value=True)
            e.tensor_reduce(colmax[:, 3:4], qkvo[:, NQKV:], AXX, ALU.max, apply_absolute_value=True)\
                .then_inc(s_wprep, 1)
            e.wait_ge(s_wpe, 1)
            link(e.tensor_reduce(m4[:, 0:1], bank[0][0:4, 0, 0:P], AXX, ALU.max))
            link(e.tensor_scalar(m4[:, 1:2], m4[:, 0:1], 1e-30, None, ALU.max))
            link(e.tensor_scalar(m4[:, 2:3].bitcast(i32), m4[:, 1:2].bitcast(i32), 0x7f800000, None,
                                 ALU.bitwise_and))
            e.tensor_scalar(m4[:, 3:4], m4[:, 2:3], 2.0, None, ALU.mult).then_inc(s_wprep, 1)
            e.wait_ge(s_wpe, 2)
            link(e.tensor_copy(pw[:, :], bank[1][:, 0, 0:4]))
            link(e.tensor_scalar(ipw[:, :].bitcast(i32), pw[:, :].bitcast(i32), -1.0,
                                 float(0x7f000000), ALU.mult, ALU.add))
            link(e.tensor_scalar(w_flt[:, 0:2 * NJ, :], w_flt[:, 0:2 * NJ, :], ipw[:, 0:1], None,
                                 ALU.mult))
            link(e.tensor_scalar(w_flt[:, 2 * NJ:, :], w_flt[:, 2 * NJ:, :], ipw[:, 1:2], None,
                                 ALU.mult))
            link(e.tensor_copy(w_nat[:, 0, :, :], w_flt[:, :, :]))
            link(e.tensor_tensor(w_nat[:, 1, :, :], w_flt[:, :, :], w_nat[:, 0, :, :], ALU.subtract))
            e.tensor_reduce(lomax[:, :], w_nat[:, 1, :, :].rearrange("p a b -> p (a b)"), AXX,
                            ALU.max, apply_absolute_value=True).then_inc(s_wprep, 1)
            e.wait_ge(s_wpe, 3)
            link(e.tensor_reduce(lo1[:, :], bank[1][0:1, 1, 0:P], AXX, ALU.max))
            e.tensor_scalar(loflag[:, :], lo1[:, :], 0.0, None, ALU.is_gt).then_inc(s_wprep, 1)
            w16 = WT[:, :, :, :].rearrange("p s j n -> p (s j) n")
            for r in range(3):
                e.wait_ge(s_wpe, 4 + r)
                lo, hi = 8 * r, min(8 * r + 8, 6 * NJ)
                src = bank[2 + r // 2][:, r % 2, :].bitcast(f16).rearrange("p (j n) -> p j n", n=P)
                e.tensor_copy(w16[:, lo:hi, :], src[:, 0:hi - lo, :])
            link(e.tensor_scalar(qkvo[:, 0:NQKV], qkvo[:, 0:NQKV], ipw[:, 2:3], None, ALU.mult))
            link(e.tensor_scalar(qkvo[:, NQKV:], qkvo[:, NQKV:], ipw[:, 3:4], None, ALU.mult))
            link(e.tensor_copy(QKVO[:, 0, :], qkvo[:, :]))
            link(e.tensor_tensor(QKVO[:, 1, :], qkvo[:, :], QKVO[:, 0, :], ALU.subtract))
            link(e.tensor_scalar(k_silu[:, :], pw[:, 0:1], 1.0 / 127.0, None, ALU.mult))
            link(e.reciprocal(k_isilu[:, :], k_silu[:, :]))
            link(e.tensor_scalar(k_ffn[:, :], k_silu[:, :], k_silu[:, 0:1], 0.5 / 127.0, ALU.mult,
                                 ALU.mult))
            link(e.tensor_scalar(k_ffn[:, :], k_ffn[:, :], pw[:, 1:2], None, ALU.mult))
            link(e.tensor_scalar(k_lim[:, :], ipw[:, 2:3], ipw[:, 2:3], None, ALU.mult))
            link(e.tensor_scalar(k_lim[:, :], k_lim[:, :], (L2_MIN / QSCALE) ** 2, 1e-37, ALU.mult,
                                 ALU.max))
            link(e.tensor_scalar(k_wo[:, :], gate_t[:, :], pw[:, 2:3], pw[:, 3:4], ALU.mult, ALU.mult))
            e.wait_ge(s_kact, 1)
            e.tensor_scalar(k_exp[:, :], k_exp[:, :], 1.0 / (QSCALE * QSCALE), None, ALU.mult)\
                .then_inc(s_wready, 1)
            e.wait_ge(s_const, 2)
            ffn_dve(e, 0)
            att_dve(e)
            ffn_dve(e, 1)

        @block.tensor
        def _(e):
            e.wait_ge(s_const, 2)
            e.wait_ge(s_wprep, 1)
            e.matmul(bank[0][0:4, 0, 0:P], colmax[:, :], ident32[:, :], is_transpose=True,
                     start=True, stop=True).then_inc(s_wpe, 1)
            e.wait_ge(s_wprep, 2)
            e.matmul(bank[1][:, 0, 0:4], m4[:, 3:4].to_broadcast([4, P]), ident32[0:4, 0:4],
                     start=True, stop=True).then_inc(s_wpe, 1)
            e.wait_ge(s_wprep, 3)
            e.matmul(bank[1][0:1, 1, 0:P], lomax[:, :], ident32[:, :], is_transpose=True,
                     start=True, stop=True).then_inc(s_wpe, 1)
            blocks = [(s, j) for s in range(2) for j in range(3 * NJ)]
            for r in range(3):
                dst = bank[2 + r // 2][:, r % 2, :].bitcast(f16)
                for a, (s, j) in enumerate(blocks[8 * r:8 * r + 8]):
                    i = e.transpose(dst[:, a * P:(a + 1) * P], w_nat[:, s, j, :], ident16[:, :])
                i.then_inc(s_wpe, 1)
            e.wait_ge(s_wready, 1)
            low = e.value_load(loflag[0:1, 0:1], min_val=0, max_val=1)

            def ffn(ph):
                with e.If(low > 0):
                    ffn_pe(e, ph, 1)
                with e.Else():
                    ffn_pe(e, ph, 0)
            ffn(0)
            e.wait_ge(s_res, NC)
            att_pe(e)
            await_read(e, B, B, ("wo", 1))
            ffn(1)


_INS = ["L0_attn_x", "L0_attn_norm_w", "L0_attn_Wq", "L0_attn_Wk", "L0_attn_Wv", "L0_attn_Wo",
        "L0_attn_gate", "L0_attn_log_temperature", "L0_ffn_w_gate", "L0_ffn_w_up", "L0_ffn_w_down"]


def kernel(**inputs):
    import numpy as _np
    import concourse.bacc as _bacc
    from concourse.bass_utils import run_bass_kernel_spmd as _run

    nc = _bacc.Bacc("TRN2", target_bir_lowering=False, num_devices=1)
    arrays, args = {}, []
    for name in _INS:
        a = _np.ascontiguousarray(inputs[name])
        if a.ndim == 0:
            a = a.reshape(1)
        arrays[f"in_{name}"] = a
        args.append(nc.dram_tensor(f"in_{name}", a.shape, mybir.dt.from_np(a.dtype),
                                   kind="ExternalInput").ap())
    shape = arrays["in_L0_attn_x"].shape
    args.append(nc.dram_tensor("result", shape, mybir.dt.float32, kind="ExternalOutput").ap())
    macaron_kernel(nc, *args)
    r = _run(nc, [arrays], core_ids=[0])
    return r.results[0]["result"]
```

```python
import concourse.bass as bass
from concourse import mybir
from contextlib import ExitStack

dt = mybir.dt
ALU = mybir.AluOpType
ACT = mybir.ActivationFunctionType
AXX = mybir.AxisListType.X


def macaron_kernel(nc, x, norm_w, wq, wk, wv, wo, gate, log_temp, w_gate, w_up, w_down, out):
    f32, f16, bf16, i32 = dt.float32, dt.float16, dt.bfloat16, dt.int32
    P = 128
    B, L, D = x.shape
    HID = w_gate.shape[0]
    NJ = HID // P
    DQ, DK = wq.shape[1], wk.shape[1]
    HD = 32
    NH, NKV = DQ // HD, DK // HD
    NQK = NH + NKV
    TPC = 4
    CH = TPC * P
    NT = B * L // P
    NC = NT // TPC
    TPB = L // P
    QCS = L // CH
    LN_EPS, RMS_EPS, L2_MIN = 1e-5, 1e-6, 1e-12
    QSCALE = 64.0
    HOT = 32.0
    MASKED = -3e38

    xt = x.rearrange("b l d -> (b l) d").rearrange("(t p) d -> p t d", p=P)
    ot = out.rearrange("b l d -> (b l) d").rearrange("(t p) d -> p t d", p=P)

    ctx = ExitStack()
    with ctx:
        def sb(name, shape, d=f32):
            return ctx.enter_context(nc.sbuf_tensor(name, shape, d))

        def sem(name):
            return ctx.enter_context(nc.semaphore(name))

        X = sb("X", [P, NT, D])
        ident16 = sb("ident16", [P, P], f16)
        ident32 = sb("ident32", [P, P])
        causal = sb("causal", [P, P], bf16)
        ones32 = sb("ones32", [P, HD])
        eps_ln = sb("eps_ln", [P, TPC])
        eps_rms = sb("eps_rms", [P, TPC])
        one = sb("one", [P, TPC])
        nhalf = sb("nhalf", [P, TPC * NQK])
        w_int = sb("w_int", [P, 3 * NJ, P], i32)
        w_flt = sb("w_flt", [P, 3 * NJ, P])
        w_nat = sb("w_nat", [P, 2, 3 * NJ, P], f16)
        WT = sb("WT", [P, 2, 3 * NJ, P], f16)
        qkvo = sb("qkvo", [P, DQ + 2 * DK + D])
        QKVO = sb("QKVO", [P, 2, DQ + 2 * DK + D], f16)
        NQKV = DQ + 2 * DK
        normw = sb("normw", [P, 1])
        colmax = sb("colmax", [P, 4])
        m4 = sb("m4", [4, 4])
        pw = sb("pw", [P, 4])
        ipw = sb("ipw", [P, 4])
        lomax = sb("lomax", [P, 1])
        lo1 = sb("lo1", [1, 1])
        loflag = sb("loflag", [1, 1], i32)
        hotflag = sb("hotflag", [1, 1], i32)
        k_silu = sb("k_silu", [P, 1])
        k_isilu = sb("k_isilu", [P, 1])
        k_ffn = sb("k_ffn", [P, 1])
        k_lim = sb("k_lim", [P, 1])
        k_exp = sb("k_exp", [P, 1])
        k_wo = sb("k_wo", [P, 1])
        gate_t = sb("gate_t", [P, 1])
        lt_t = sb("lt_t", [P, 1])
        bns = sb("bns", [P, TPC, 6])
        MV = [sb(f"MV{i}", [P, TPC, 2]) for i in range(2)]
        RS = [sb(f"RS{i}", [P, TPC]) for i in range(2)]
        XN = [sb(f"XN{i}", [P, TPC, P]) for i in range(2)]
        XS = [sb(f"XS{i}", [P, 2, TPC, P], f16) for i in range(2)]
        XT = [sb(f"XT{i}", [P, 2, CH], f16) for i in range(2)]
        SG = [sb(f"SG{i}", [P, CH]) for i in range(NJ)]
        H = [sb(f"H{i}", [P, CH]) for i in range(NJ)]
        HH = [sb(f"HH{i}", [P, NJ, CH], f16) for i in range(2)]
        HL = [sb(f"HL{i}", [P, NJ, CH], f16) for i in range(2)]
        AMV = [sb(f"AMV{i}", [P, TPC, 2]) for i in range(2)]
        AN = [sb(f"AN{i}", [P, TPC, P]) for i in range(2)]
        AS = [sb(f"AS{i}", [P, 2, TPC, P], f16) for i in range(2)]
        rv = [sb(f"rv{i}", [P, TPC]) for i in range(2)]
        RMS = [sb(f"RMS{i}", [P, TPC]) for i in range(2)]
        A1 = [sb(f"A1{i}", [P, TPC]) for i in range(2)]
        B1 = [sb(f"B1{i}", [P, TPC]) for i in range(2)]
        SQ = sb("SQ", [P, TPC, NQK * HD])
        SS = [sb(f"SS{i}", [P, TPC, NQK]) for i in range(2)]
        R = [sb(f"R{i}", [P, TPC, NQK]) for i in range(2)]
        QN = [sb(f"QN{i}", [P, TPC, NQK, HD]) for i in range(2)]
        ST = [sb(f"ST{i}", [P, TPC, NQK, 4, HD], f16) for i in range(2)]
        QT = [sb(f"QT{i}", [P, NH, L], f16) for i in range(2)]
        KT = [sb(f"KT{i}", [P, NKV, L], f16) for i in range(2)]
        V = [sb(f"V{i}", [P, TPB, NQKV]) for i in range(2)]
        PT = [sb(f"PT{i}", [P, NH, CH]) for i in range(2)]
        PVS = sb("PVS", [P, 2, CH])
        RD = sb("RD", [P, CH])
        MX = sb("MX", [P, 2, TPC, NH])
        MN = sb("MN", [P, TPC, NH])
        bridge = sb("bridge", [P, 1])
        ON = sb("ON", [P, CH])
        OH = sb("OH", [P, CH], f16)
        OL = sb("OL", [P, CH], f16)

        bank = [ctx.enter_context(nc.psum_tensor(f"bank{i}", [P, 2, CH], f32)) for i in range(4)]
        GU = bank[0:NJ]
        XP = bank[3][:, 0, :].bitcast(f16).rearrange("p (s n) -> p s n", s=2)
        DN = bank[3][:, 1, :].rearrange("p (t d) -> p t d", t=TPC)
        SCORES = bank[0:2]
        PVD = bank[2][:, :, :]
        MB = [bank[3][:, i, :] for i in range(2)]

        w_bank = [bank[2][:, 0, :], bank[2][:, 1, :], bank[0][:, 1, :]]

        s_xl = [sem(f"s_xl{i}") for i in range(2)]
        s_xin = [sem(f"s_xin{i}") for i in range(2)]
        (s_w, s_wo_in, s_one, s_wready, s_wprep, s_wt, s_wpe, s_kact, s_const) = [sem("s_" + n) for n in (
            "w", "wo_in", "one", "wready", "wprep", "wt", "wpe", "kact", "const")]
        (s_stat, s_rstd, s_xn, s_xh, s_xp, s_xt, s_gu, s_silu, s_h, s_hh, s_hl, s_dn,
         s_res, s_out) = [sem("s_" + n) for n in (
            "stat", "rstd", "xn", "xh", "xp", "xt", "gu", "silu", "h", "hh", "hl", "dn",
            "res", "out")]
        (a_stat, a_rstd, a_coef, a_xn, a_y, a_xh, a_xl, a_sq, a_ss, a_r, a_qn, a_hi, a_h2, a_lo, a_full,
         a_free, a_cp, a_s, a_exp, a_pv, a_pvc, a_rd, a_on, a_oh, a_ol, a_mx) = [sem("a_" + n) for n in (
            "stat", "rstd", "coef", "xn", "y", "xh", "xl", "sq", "ss", "r", "qn", "hi", "h2", "lo",
            "full", "free", "cp", "s", "exp", "pv", "pvc", "rd", "on", "oh", "ol", "mx")]

        block = ctx.enter_context(nc.Block())

        def drive(eng, step, n, head, tail):
            for i in range(head):
                step(i, i)
            with eng.Fori(0, (n - head - tail) // 2) as it:
                for u in range(2):
                    step(head + u, it * 2 + (head + u))
            for i in range(n - tail, n):
                step(i, i)

        def pipeline(eng, ops, early=(), after={}):
            lo, hi = min(o for o, _ in ops), max(o for o, _ in ops)
            first = 2 - lo
            first += (NC - hi - first) % 2

            def step(k, c):
                for off, op in ops:
                    if 0 <= k + off < NC and (op, k + off) not in early:
                        op(k + off, c + off)
            for i in range(-hi, first):
                step(i, i)
            with eng.Fori(0, (NC - hi - first) // 2) as it:
                for u in range(2):
                    step(first + u, it * 2 + (first + u))
            for i in range(NC - hi, NC - lo):
                step(i, i)
                if i in after:
                    after[i]()

        def tiles(c):
            return X[:, bass.ds(c * TPC, TPC), :] if not isinstance(c, int) else \
                X[:, c * TPC:(c + 1) * TPC, :]

        def tile(c, t):
            if isinstance(c, int):
                return X[:, c * TPC + t, :]
            return X[:, bass.ds(c * TPC + t, 1), :].rearrange("p t d -> p (t d)")

        def ffn_x_lo(e, k, c, ph, parity):
            if k % 2 != parity:
                return
            e.wait_ge(s_xh, c + NC * ph + 1)
            e.tensor_tensor(XS[k % 2][:, 1, :, :], XN[k % 2][:, :, :], XS[k % 2][:, 0, :, :],
                            ALU.subtract).then_inc(s_xl[k % 2], 2)

        def ffn_dve(e, ph, when, after={}):
            def stats(k, c):
                if ph == 0:
                    e.wait_ge(s_xin[k % 2], (c - k % 2) * 8 + 16)
                g = c + NC * ph
                if k >= 1 or ph:
                    e.wait_ge(s_stat, 2 * g)
                for t in range(TPC):
                    i = e.bn_stats(bns[:, t, :], tile(c, t))
                i.then_inc(s_stat, 1)

            def sums_there(k, c):
                e.wait_ge(s_stat, 2 * (c + NC * ph) + 1)

            def aggregate(k, c):
                for t in range(TPC):
                    i = e.bn_aggr(MV[k % 2][:, t, :], bns[:, t, :])
                i.then_inc(s_stat, 1)

            def normalise(k, c):
                g = c + NC * ph
                e.wait_ge(s_rstd, 2 * g + 2)
                if k >= 2 or ph:
                    e.wait_ge(s_xl[k % 2], g - k % 2)
                for t in range(TPC):
                    i = e.tensor_scalar(XN[k % 2][:, t, :], tile(c, t), MV[k % 2][:, t, 0:1],
                                        RS[k % 2][:, t:t + 1], ALU.subtract, ALU.mult)
                i.then_inc(s_xn, 1)

            def hidden(k, c, j):
                n = (c + NC * ph) * NJ + j
                e.wait_ge(s_silu, n + 1)
                if k >= 1 or ph:
                    e.wait_ge(s_hh, n - NJ + 1)
                    e.wait_ge(s_hl, n - NJ + 1)
                e.scalar_tensor_tensor(H[j][:, :], SG[j][:, :], k_isilu[:, 0:1], GU[j][:, 1, :],
                                       ALU.mult, ALU.mult).then_inc(s_h, 1)

            def residual(k, c):
                e.wait_ge(s_dn, c + NC * ph + 1)
                e.scalar_tensor_tensor(tiles(c), DN, k_ffn[:, 0:1], tiles(c),
                                       ALU.mult, ALU.add).then_inc(s_res, 1)

            def x_lo(k, c):
                ffn_x_lo(e, k, c, ph, 1)
            stages = (stats, sums_there, aggregate)
            if ph:
                early = [[(op, c) for c in range(2) for op in stages] + [(normalise, 0)] +
                         [(op, 2) for op in stages] + [(normalise, 1)]]
            else:
                early = [[(op, 0) for op in stages] + [(normalise, 0)], [(op, 1) for op in stages]]
            if when < 1:
                for op, c in early[int(2 * when)]:
                    op(c, c)
                return
            early = sum(early, [])
            pipeline(e, [(4, stats), (0, lambda k, c: hidden(k, c, 1)),
                         (2, x_lo),
                         (4, sums_there), (0, lambda k, c: hidden(k, c, 2)), (4, aggregate),
                         (3, normalise),
                         (-1, residual), (1, lambda k, c: hidden(k, c, 0))], early, after)

        def ffn_pool(e, ph, when, after={}):
            def rstd(k, c):
                g = c + NC * ph
                e.wait_ge(s_stat, 2 * g + 2)
                if k >= 2 or ph:
                    e.wait_ge(s_xn, g - 1)
                e.tensor_tensor(RS[k % 2][:, :], MV[k % 2][:, :, 1], eps_ln[:, :], ALU.add)\
                    .then_inc(s_rstd, 1)
                e.wait_ge(s_rstd, 2 * g + 1)
                e.tensor_tensor(RS[k % 2][:, :], RS[k % 2][:, :], nhalf[:, 0:TPC], ALU.pow)\
                    .then_inc(s_rstd, 1)

            def h_lo(k, c, j):
                n = (c + NC * ph) * NJ + j
                e.wait_ge(s_hh, n + 1)
                e.tensor_tensor(HL[k % 2][:, j, :], H[j][:, :], HH[k % 2][:, j, :],
                                ALU.subtract).then_inc(s_hl, 1)

            def x_lo(k, c):
                ffn_x_lo(e, k, c, ph, 0)
            early = [(rstd, 0), (rstd, 1), (x_lo, 0)] if ph else [(rstd, 0), (x_lo, 0), (rstd, 1)]
            if when == 0:
                for op, c in early:
                    op(c, c)
                return
            pipeline(e, [(3, rstd), (2, x_lo)] +
                     [(0, lambda k, c, j=j: h_lo(k, c, j)) for j in range(NJ)], early, after)

        def ffn_act(e, ph, when, after={}):
            def x_hi(k, c):
                g = c + NC * ph
                e.wait_ge(s_xn, g + 1)
                if k >= 2 or ph:
                    e.wait_ge(s_xp, g - 1)
                e.activation(XS[k % 2][:, 0, :, :], XN[k % 2][:, :, :], ACT.Copy).then_inc(s_xh, 1)

            def xt_out(k, c):
                e.wait_ge(s_xp, c + NC * ph + 1)
                e.activation(XT[k % 2][:, :, :], XP, ACT.Copy).then_inc(s_xt, 1)

            def silu(k, c, j):
                n = (c + NC * ph) * NJ + j
                e.wait_ge(s_gu, n + 1)
                if k >= 1 or ph:
                    e.wait_ge(s_h, n - NJ + 1)
                e.activation(SG[j][:, :], GU[j][:, 0, :], ACT.Silu, scale=k_silu[:, 0:1])\
                    .then_inc(s_silu, 1)

            def h_hi(k, c, j):
                n = (c + NC * ph) * NJ + j
                e.wait_ge(s_h, n + 1)
                if j == 0 and (k >= 2 or ph):
                    e.wait_ge(s_dn, c + NC * ph - 1)
                e.activation(HH[k % 2][:, j, :], H[j][:, :], ACT.Copy)\
                    .then_inc(s_hh, 1)

            early = [(x_hi, 0), (x_hi, 1)] if ph else [(x_hi, 0)]
            if when == 0:
                for op, c in early:
                    op(c, c)
                return

            def op(f, j):
                return lambda k, c: f(k, c, j)
            pipeline(e, [(2, x_hi), (0, op(silu, 1)), (0, op(h_hi, 0)), (0, op(silu, 2)),
                         (0, op(h_hi, 1)), (1, op(silu, 0)), (0, op(h_hi, 2)), (2, xt_out)],
                     early, after)

        def ffn_pe(e, ph, low, when=1):
            def x_t(k, c):
                g = c + NC * ph
                e.wait_ge(s_xl[k % 2], g - k % 2 + 2)
                if k >= 1 or ph:
                    e.wait_ge(s_xt, g)
                for part in range(2):
                    for t in range(TPC):
                        i = e.transpose(XP[:, part, t * P:(t + 1) * P], XS[k % 2][:, part, t, :],
                                        ident16[:, :])
                i.then_inc(s_xp, 1)

            def gate_up(k, c, j):
                n = (c + NC * ph) * NJ + j
                if j == 0:
                    e.wait_ge(s_xt, c + NC * ph + 1)
                if k >= 1 or ph:
                    e.wait_ge(s_h, n - NJ + 1)
                for w in range(2):
                    passes = [(0, 0), (0, 1)] + [(1, 0)] * low
                    for a, (wp, xp) in enumerate(passes):
                        i = e.matmul(GU[j][:, w, :], WT[:, wp, w * NJ + j, :], XT[k % 2][:, xp, :],
                                     start=a == 0, stop=a == len(passes) - 1)
                i.then_inc(s_gu, 1)

            def down(k, c):
                g = c + NC * ph
                e.wait_ge(s_hl, (g + 1) * NJ)
                if k >= 1 or ph:
                    e.wait_ge(s_res, g)
                for t in range(TPC):
                    passes = [(hp, wp, j) for hp, wp in [(0, 0), (1, 0)] + [(0, 1)] * low
                              for j in range(NJ)]
                    for a, (hp, wp, j) in enumerate(passes):
                        i = e.matmul(DN[:, t, :],
                                     (HH, HL)[hp][k % 2][:, j, t * P:(t + 1) * P],
                                     WT[:, wp, 2 * NJ + j, :], start=a == 0,
                                     stop=a == len(passes) - 1)
                i.then_inc(s_dn, 1)

            early = [(x_t, 0)]
            if when == 0:
                x_t(0, 0)
                return
            pipeline(e, [(1, x_t), (0, lambda k, c: gate_up(k, c, 1)),
                         (0, lambda k, c: gate_up(k, c, 2)), (1, lambda k, c: gate_up(k, c, 0)),
                         (-1, down)], early)

        groups = [(qc, i) for qc in range(QCS) for i in range(TPC * (qc + 1))]
        NG = len(groups)
        G0 = TPC

        USES = {0: [("x", 0), ("x", 1)], 1: [("qkv", 0, 0), ("qkv", 0, 1)],
                2: [("qkv", 1, 0), ("qkv", 1, 1)], 3: [("wo", 1)],
                7: [("t", 0, 0), ("t", 0, 1)], 8: [("t", 0, 2), ("wo", 0)],
                10: [("t", 1, 0), ("t", 1, 1)], 11: [("t", 1, 2)]}
        MOVED = {0: [], 1: [], 2: USES[0], 3: USES[1], 4: USES[2]}
        FIRST = [("x", 0), ("x", 1)] + [("qkv", h, c) for h in range(2) for c in range(2)] + \
                [("t", 0, j) for j in range(3)]
        LATE = [("t", 1, j) for j in range(3)]

        def row_uses(half):
            return [("m", half, h, t, kb) for h in range(NH) for t in range(TPC)
                    for kb in range(half + 1)] + [("u", half, j) for j in range(2)]

        def bank_uses(shift):
            def planned(us):
                return [v for u in us
                        for v in [u] + (row_uses(u[1]) if shift and u[0] == "t" and u[2] == 2 else [])]

            def uses_in(k, g):
                us = MOVED.get(g, USES.get(g, [])) if k == 0 else USES.get(g, [])
                return planned([u for u in us if not (u[0] != "wo" and k == B - 1)
                                and not (u == ("wo", 1) and k == 0)])

            seq = [(None, u) for u in planned(FIRST) + planned(LATE)] + \
                  [(k, u) for k in range(B) for g in range(NG) for u in uses_in(k, g)] + \
                  [(B, ("wo", 1))]
            reads = {a_cp: 0, a_free: 0}
            USE = {}
            for n, (k, u) in enumerate(seq):
                s = a_cp if u[0] == "qkv" else a_free
                reads[s] += 1
                USE[k, u] = (n, s, reads[s])
            in_batch = [u for g in range(NG) for u in uses_in(1, g)]
            PER = {a_cp: sum(u[0] == "qkv" for u in in_batch),
                   a_free: sum(u[0] != "qkv" for u in in_batch), a_full: len(in_batch)}

            def at_batch(s, k, b, v):
                return v if k is None or isinstance(b, int) else v + (b - k) * PER[s]

            def await_full(e, k, b, u):
                n = USE[k, u][0]
                e.wait_ge(a_full, at_batch(a_full, k, b, n + 1))
                return MB[n % 2]

            def await_read(e, k, b, u):
                n, s, v = USE[k, u]
                e.wait_ge(s, at_batch(s, k, b, v))
            return uses_in, await_full, await_read, seq, USE

        def width(g):
            qc, i = groups[g]
            return CH - max(0, i - TPC * qc) * P

        def att_pe(e, shift):
            uses_in, _, await_read, seq, USE = bank_uses(shift)

            def scores(k, b, g, hp):
                qc, i = groups[g]
                n = width(g)
                q0 = (qc + 1) * CH - n
                G = b * NG + g
                if k * NG + g >= 1:
                    e.wait_ge(a_exp, 2 * G + hp - 1)
                if hp == 0 and i == 0:
                    u = ("u", qc, 1) if shift else ("t", qc, 2)
                    await_read(e, *((k - 1, b - 1) if k else (None, None)), u)
                diag = i >= TPC * qc
                for h in range(2):
                    o = SCORES[hp][:, h, 0:n]
                    i_ = e.matmul(o, KT[k % 2][:, hp, i * P:(i + 1) * P],
                                  QT[k % 2][:, 2 * hp + h, q0:q0 + n], start=True, stop=True)
                if diag:
                    for h in range(2):
                        i_ = e.matmul(SCORES[hp][:, h, 0:P], ident16[:, :], causal[:, :], start=False,
                                      stop=True, skip_group_check=True)
                i_.then_inc(a_s, 1)

            def weigh(k, b, g):
                qc, i = groups[g]
                n = width(g)
                G = b * NG + g
                e.wait_ge(a_exp, 2 * G + 2)
                again = i == 0 and k * QCS + qc >= 1
                if again:
                    e.wait_ge(a_pvc, 2 * (b * QCS + qc) - 1)
                done = i >= TPC * qc
                for h in range(NH):
                    v0 = DQ + DK + HD * (h // 2)
                    e.matmul(PVD[HD * h:HD * h + HD, 0, CH - n:CH], V[k % 2][:, i, v0:v0 + HD],
                             PT[g % 2][:, h, 0:n], start=i == 0, stop=done, skip_group_check=True)
                if again:
                    e.wait_ge(a_pvc, 2 * (b * QCS + qc))
                for h in range(NH):
                    i_ = e.matmul(PVD[HD * h:HD * h + HD, 1, CH - n:CH], ones32[:, :],
                                  PT[g % 2][:, h, 0:n], start=i == 0, stop=done,
                                  skip_group_check=True)
                i_.then_inc(a_pv, 1)

            def use(k, b, u):
                rb = 0 if k is None else b + 1 if u[0] != "wo" else b - u[1]
                n = USE[k, u][0]
                q = n % 2
                if n >= 2:
                    pk, pu = seq[n - 2]
                    if k is None or isinstance(b, int):
                        await_read(e, pk, pk, pu)
                    else:
                        await_read(e, pk, b + (pk - k), pu)
                m16 = MB[q].bitcast(f16)
                if u[0] == "x":
                    half = u[1]
                    e.wait_ge(a_xl, rb * 2 + half + 1)
                    for part in range(2):
                        for t in range(TPC):
                            i_ = e.transpose(m16[:, (part * TPC + t) * P:(part * TPC + t + 1) * P],
                                             AS[half][:, part, t, :], ident16[:, :])
                elif u[0] == "qkv":
                    half = u[1]
                    await_read(e, k, b, ("x", half))
                    for t in range(2):
                        tt = 2 * u[2] + t
                        for a, (xp, wp) in enumerate([(0, 0), (1, 0), (0, 1)]):
                            i_ = e.matmul(MB[q][:, t * NQKV:(t + 1) * NQKV],
                                          XT[half][:, xp, tt * P:(tt + 1) * P],
                                          QKVO[:, wp, 0:NQKV], start=a == 0, stop=a == 2)
                elif u[0] in "tu":
                    if u[0] == "t":
                        e.wait_ge(a_lo, rb * 2 + u[1] + 1)
                        e.wait_ge(a_h2, rb * 2 + u[1] + 1)
                    else:
                        e.wait_ge(a_mx, (rb * 2 + u[1] + 1) * 3)
                    for h in range(2):
                        for t in range(TPC):
                            i_ = e.transpose(
                                m16[:, (h * TPC + t) * P:(h * TPC + t + 1) * P],
                                ST[u[1]][:, t, 2 * u[2] + h, :, :].rearrange("p s d -> p (s d)"),
                                ident16[:, :])
                elif u[0] == "m":
                    half, h, t, kb = u[1:]
                    if (h, t, kb) == (0, 0, 0):
                        await_read(e, k, b, ("t", half, 2))
                    kp = 0 if k is None else (k + 1) % 2
                    n_ = CH if kb < half else (t + 1) * P
                    i_ = e.matmul(MB[q][:, 0:n_], QT[kp][:, h, half * CH + t * P:half * CH + t * P + P],
                                  KT[kp][:, h // 2, kb * CH:kb * CH + n_], start=True, stop=True)
                    if kb == half:
                        i_ = e.matmul(MB[q][:, t * P:(t + 1) * P], causal[:, :], ident16[:, :],
                                      start=False, stop=True, skip_group_check=True)
                else:
                    e.wait_ge(a_ol, rb * 2 + u[1] + 1)
                    for t in range(TPC):
                        for a, (o_, wp) in enumerate([(OH, 0), (OL, 0), (OH, 1)]):
                            i_ = e.matmul(MB[q][:, t * P:(t + 1) * P], o_[:, t * P:(t + 1) * P],
                                          QKVO[:, wp, NQKV:], start=a == 0, stop=a == 2)
                i_.then_inc(a_full, 1)

            first = [u for k, u in seq if k is None and u[:2] not in (("t", 1), ("m", 1), ("u", 1))]
            late = [u for k, u in seq if k is None and u not in first]
            for u in first:
                use(None, None, u)
            scores(0, 0, 0, 0)
            scores(0, 0, 0, 1)

            def step(k, b):
                for g in range(NG):
                    if g + 1 < NG:
                        scores(k, b, g + 1, 0)
                        scores(k, b, g + 1, 1)
                    elif k + 1 < B:
                        scores(k + 1, b + 1, 0, 0)
                        scores(k + 1, b + 1, 0, 1)
                    weigh(k, b, g)
                    if k == 0 and g == 0:
                        for u in late:
                            use(None, None, u)
                    for u in uses_in(k, g):
                        use(k, b, u)
            drive(e, step, B, 1, 3)
            use(B, B, ("wo", 1))
            await_read(e, B, B, ("wo", 1))

        def att_act(e, shift, first=None):
            _, await_full, await_read, _, _ = bank_uses(shift)

            def exps(k, b, g):
                n = width(g)
                G = b * NG + g
                for hp in range(2):
                    e.wait_ge(a_s, 2 * G + hp + 1)
                    if hp == 0 and k * NG + g >= 2:
                        e.wait_ge(a_pv, G - 1)
                    e.activation(PT[g % 2][:, 2 * hp:2 * hp + 2, 0:n], SCORES[hp][:, :, 0:n], ACT.Exp,
                                 scale=k_exp[:, 0:1]).then_inc(a_exp, 1)

            def x_hi(m, half, k, b):
                e.wait_ge(a_xn, m + 1)
                if m is not half:
                    await_full(e, k, b, ("x", half))
                e.activation(AS[half][:, 0, :, :], AN[half][:, :, :], ACT.Copy).then_inc(a_xh, 1)

            def qkv_out(kk, m, k, b, half):
                for c in range(2):
                    src = await_full(e, k, b, ("qkv", half, c))
                    t0 = half * TPC + 2 * c
                    e.activation(V[kk % 2][:, t0:t0 + 2, :], src.rearrange("p (t n) -> p t n", t=2),
                                 ACT.Copy).then_inc(a_cp, 1)
                await_read(e, k, b, ("qkv", half, 1))
                t0 = half * TPC
                if not (isinstance(m, int) and m < 1):
                    e.wait_ge(a_ss, 2 * m - 1)
                e.activation(SQ[:, :, :], V[kk % 2][:, t0:t0 + TPC, 0:DQ + DK], ACT.Square)\
                    .then_inc(a_sq, 1)

            def stack_hi(m, half):
                e.wait_ge(a_qn, m + 1)
                e.activation(ST[half][:, :, :, 0, :], QN[half][:, :, :, :], ACT.Copy).then_inc(a_hi, 1)

            def o_hi(m):
                e.wait_ge(a_on, m + 1)
                e.activation(OH[:, :], ON[:, :], ACT.Copy).then_inc(a_oh, 1)

            def pv_out(m, G, first=False):
                e.wait_ge(a_pv, G)
                if not first:
                    e.wait_ge(a_on, m)
                for i in range(2):
                    e.activation(PVS[:, i, :], PVD[:, i, :], ACT.Copy).then_inc(a_pvc, 1)

            if first is not None:
                x_hi(first[1], first[1], None, None)
                return
            for half in range(2):
                qkv_out(0, half, None, None, half)
            stack_hi(0, 0)
            exps(0, 0, 0)
            stack_hi(1, 1)

            def step(k, b):
                m0 = 2 * (b + 1)
                for g in range(NG):
                    if g == 0 and k >= 1:
                        pv_out(b * 2 - 1, b * NG)
                    if g == G0:
                        pv_out(b * 2, b * NG + G0, k == 0)
                    if g + 1 < NG:
                        exps(k, b, g + 1)
                    elif k + 1 < B:
                        exps(k + 1, b + 1, 0)
                    if g == 2 and k >= 1:
                        o_hi(b * 2 - 1)
                    if g == 6:
                        o_hi(b * 2)
                    if k + 1 < B:
                        if k == 0 and g == 1:
                            for half in range(2):
                                x_hi(2 + half, half, None, None)
                        g_ = g - 2 if k == 0 else g
                        if g_ in (1, 2):
                            qkv_out(k + 1, m0 + (g_ == 2), k, b, int(g_ == 2))
                        if g in (5, 7):
                            stack_hi(m0 + (g == 7), int(g == 7))
                    if k + 2 < B and g in (9, 10):
                        x_hi(m0 + 2 + (g == 10), int(g == 10), k, b)
            drive(e, step, B, 1, 3)
            pv_out(B * 2 - 1, B * NG)
            ffn_act(e, 1, 0)
            o_hi(B * 2 - 1)

        def att_pool(e, first=None):
            def rstds(m, half):
                e.wait_ge(a_stat, 2 * m + 2)
                if not (isinstance(m, int) and m < 2):
                    e.wait_ge(a_y, m - 1)
                e.tensor_tensor(rv[half][:, :], AMV[half][:, :, 1], eps_ln[:, :], ALU.add).then_inc(a_coef, 1)
                e.wait_ge(a_coef, 5 * m + 1)
                e.tensor_tensor(RMS[half][:, :], rv[half][:, :], eps_rms[:, :], ALU.mult).then_inc(a_coef, 1)
                e.wait_ge(a_coef, 5 * m + 2)
                e.tensor_tensor(RMS[half][:, :], RMS[half][:, :], AMV[half][:, :, 1], ALU.add)
                e.tensor_tensor(rv[half][:, :], rv[half][:, :], nhalf[:, 0:TPC], ALU.pow).then_inc(a_coef, 1)
                e.wait_ge(a_coef, 5 * m + 3)
                e.tensor_tensor(RMS[half][:, :], RMS[half][:, :], nhalf[:, 0:TPC], ALU.pow).then_inc(a_rstd, 1)
                e.tensor_tensor(A1[half][:, :], rv[half][:, :], one[:, :], ALU.add).then_inc(a_coef, 1)
                e.tensor_tensor(B1[half][:, :], rv[half][:, :], AMV[half][:, :, 0], ALU.mult).then_inc(a_coef, 1)

            def x_lo(m, half):
                e.wait_ge(a_xh, m + 1)
                e.tensor_tensor(AS[half][:, 1, :, :], AN[half][:, :, :], AS[half][:, 0, :, :],
                                ALU.subtract).then_inc(a_xl, 1)

            def norms(m, half):
                e.wait_ge(a_ss, 2 * m + 2)
                if not (isinstance(m, int) and m < 2):
                    e.wait_ge(a_qn, m - 1)
                e.tensor_tensor(R[half][:, :, :], SS[half][:, :, :],
                                nhalf[:, :].rearrange("p (t h) -> p t h", t=TPC), ALU.pow)\
                    .then_inc(a_r, 1)

            def stack_lo(m, half):
                e.wait_ge(a_hi, m + 1)
                e.tensor_tensor(ST[half][:, :, 0:NH, 2, :], QN[half][:, :, 0:NH, :],
                                ST[half][:, :, 0:NH, 0, :], ALU.subtract)
                e.tensor_tensor(ST[half][:, :, NH:NQK, 1, :], QN[half][:, :, NH:NQK, :],
                                ST[half][:, :, NH:NQK, 0, :], ALU.subtract).then_inc(a_lo, 1)

            def o_lo(m):
                e.wait_ge(a_oh, m + 1)
                e.tensor_tensor(OL[:, :], ON[:, :], OH[:, :], ALU.subtract).then_inc(a_ol, 1)

            if first is not None:
                {"rstds": rstds, "x_lo": x_lo}[first[0]](first[1], first[1])
                return
            norms(0, 0)
            stack_lo(0, 0)
            norms(1, 1)
            rstds(2, 0)
            stack_lo(1, 1)
            rstds(3, 1)
            x_lo(2, 0)
            x_lo(3, 1)

            def step(k, b):
                m0 = 2 * (b + 1)
                nxt = k + 1 < B
                if k >= 1:
                    o_lo(b * 2 - 1)
                if nxt:
                    norms(m0, 0)
                    norms(m0 + 1, 1)
                    stack_lo(m0, 0)
                o_lo(b * 2)
                if k + 2 < B:
                    rstds(m0 + 2, 0)
                if nxt:
                    stack_lo(m0 + 1, 1)
                if k + 2 < B:
                    rstds(m0 + 3, 1)
                    x_lo(m0 + 2, 0)
                    x_lo(m0 + 3, 1)
            drive(e, step, B, 1, 3)
            ffn_pool(e, 1, 0)
            o_lo(B * 2 - 1)

        def att_dve(e, shift, first=None):
            _, await_full, await_read, _, _ = bank_uses(shift)

            def stats(m, c, half):
                if not (isinstance(m, int) and m < 2):
                    e.wait_ge(a_coef, 5 * m - 5)
                if not (isinstance(m, int) and m < 1):
                    e.wait_ge(a_stat, 2 * m)
                for t in range(TPC):
                    i = e.bn_stats(bns[:, t, :], tile(c, t))
                i.then_inc(a_stat, 1)
                e.wait_ge(a_stat, 2 * m + 1)
                e.memset(bridge[:, :], 0.0)
                for t in range(TPC):
                    i = e.bn_aggr(AMV[half][:, t, :], bns[:, t, :])
                i.then_inc(a_stat, 1)

            def normalise(m, c, half):
                e.wait_ge(a_rstd, m + 1)
                if not (isinstance(m, int) and m < 2):
                    e.wait_ge(a_xl, m - 1)
                for t in range(TPC):
                    i = e.tensor_scalar(AN[half][:, t, :], tile(c, t), AMV[half][:, t, 0:1],
                                        RMS[half][:, t:t + 1], ALU.subtract, ALU.mult)
                i.then_inc(a_xn, 1)

            def add_norm(m, c, half):
                e.wait_ge(a_coef, 5 * m + 5)
                e.wait_ge(a_xn, m + 1)
                for t in range(TPC):
                    i = e.tensor_scalar(tile(c, t), tile(c, t), A1[half][:, t:t + 1], B1[half][:, t:t + 1],
                                        ALU.mult, ALU.subtract)
                i.then_inc(a_y, 1)

            def xt_out(k, b, half):
                src = await_full(e, k, b, ("x", half))
                e.tensor_copy(XT[half][:, :, :], src.bitcast(f16).rearrange("p (s n) -> p s n", s=2))\
                    .then_inc(a_free, 1)

            def sums(m, half):
                e.wait_ge(a_sq, m + 1)
                if not (isinstance(m, int) and m < 2):
                    e.wait_ge(a_r, m - 1)
                e.tensor_reduce(SS[half][:, :, :], SQ[:, :, :].rearrange("p t (h d) -> p t h d", d=HD),
                                AXX, ALU.add).then_inc(a_ss, 1)
                e.wait_ge(a_ss, 2 * m + 1)
                e.tensor_scalar(SS[half][:, :, :], SS[half][:, :, :], 1.0 / (QSCALE * QSCALE), k_lim[:, 0:1],
                                ALU.mult, ALU.max).then_inc(a_ss, 1)

            def unit(kk, m, half):
                e.wait_ge(a_r, m + 1)
                if not (isinstance(m, int) and m < 2):
                    e.wait_ge(a_lo, m - 1)
                t0 = half * TPC
                e.tensor_tensor(
                    QN[half][:, :, :, :],
                    V[kk % 2][:, t0:t0 + TPC, 0:DQ + DK].rearrange("p t (h d) -> p t h d", d=HD),
                    R[half][:, :, :].unsqueeze(3).to_broadcast([P, TPC, NQK, HD]), ALU.mult)\
                    .then_inc(a_qn, 1)

            def stack_hi2(m, half):
                e.wait_ge(a_hi, m + 1)
                if shift:
                    e.memset(ST[half][:, :, 0:NH, 3, 0:2], 0.0)
                e.tensor_copy(ST[half][:, :, 0:NH, 1, :], ST[half][:, :, 0:NH, 0, :])
                e.tensor_copy(ST[half][:, :, NH:NQK, 2, :], ST[half][:, :, NH:NQK, 0, :]).then_inc(a_h2, 1)

            def t_out(kk, k, b, half, j, u="t"):
                src = await_full(e, k, b, (u, half, j)).bitcast(f16)
                src = src.rearrange("p (h n) -> p h n", h=2)
                cols = slice(half * CH, half * CH + CH)
                dst = QT[kk % 2][:, 2 * j:2 * j + 2, cols] if j < 2 else KT[kk % 2][:, :, cols]
                e.tensor_copy(dst, src).then_inc(a_free, 1)

            def transposed(kk, m, k, b, half):
                for j in range(3):
                    t_out(kk, k, b, half, j)
                if not shift:
                    return
                for _, h, t, kb in [u[1:] for u in row_uses(half) if u[0] == "m"]:
                    src = await_full(e, k, b, ("m", half, h, t, kb))
                    e.tensor_reduce(MX[:, kb, t, h:h + 1], src[:, 0:CH if kb < half else (t + 1) * P],
                                    AXX, ALU.max).then_inc(a_free, 1)
                await_read(e, k, b, ("m", half, NH - 1, TPC - 1, half))
                e.tensor_tensor(MN[:, :, :], MX[:, 0, :, :], MX[:, half, :, :], ALU.max)\
                    .then_inc(a_mx, 1)
                e.wait_ge(a_mx, 3 * m + 1)
                e.tensor_scalar(ST[half][:, :, 0:NH, 3, 0], MN[:, :, :], -1.0, None, ALU.mult)\
                    .then_inc(a_mx, 1)
                e.wait_ge(a_mx, 3 * m + 2)
                e.scalar_tensor_tensor(ST[half][:, :, 0:NH, 3, 1], MN[:, :, :], -1.0,
                                       ST[half][:, :, 0:NH, 3, 0], ALU.mult, ALU.subtract)\
                    .then_inc(a_mx, 1)
                for j in range(2):
                    t_out(kk, k, b, half, j, "u")

            def o_norm(m, first=False):
                e.wait_ge(a_pvc, 2 * m + 2)
                if not first:
                    e.wait_ge(a_ol, m)
                e.reciprocal(RD[:, :], PVS[:, 1, :]).then_inc(a_rd, 1)
                e.wait_ge(a_rd, m + 1)
                e.tensor_tensor(ON[:, :], PVS[:, 0, :], RD[:, :], ALU.mult).then_inc(a_on, 1)

            def wo_out(k, b, u, c):
                src = await_full(e, k, b, u).rearrange("p (t d) -> p t d", t=TPC)
                e.scalar_tensor_tensor(tiles(c), src, k_wo[:, 0:1], tiles(c), ALU.mult, ALU.add)\
                    .then_inc(a_free, 1)

            if first is not None:
                {"stats": stats, "normalise": normalise, "add_norm": add_norm}[first[0]](
                    first[1], first[1], first[1])
                return
            for half in range(2):
                xt_out(None, None, half)
            sums(0, 0)
            sums(1, 1)
            stats(2, 2, 0)
            stats(3, 3, 1)
            for half in range(2):
                unit(0, half, half)
                stack_hi2(half, half)
                transposed(0, half, None, None, half)
            for half in range(2):
                normalise(2 + half, 2 + half, half)
            for half in range(2):
                add_norm(2 + half, 2 + half, half)

            def step(k, b):
                m0 = (b + 1) * 2
                nxt = k + 1 < B
                if nxt:
                    xt_out(k, b, 0)
                    xt_out(k, b, 1)
                if k >= 1:
                    o_norm(b * 2 - 1)
                if nxt:
                    sums(m0, 0)
                    sums(m0 + 1, 1)
                if k >= 1:
                    wo_out(k, b, ("wo", 1), b * 2 - 1)
                if nxt:
                    unit(k + 1, m0, 0)
                o_norm(b * 2, k == 0)
                if nxt:
                    stack_hi2(m0, 0)
                    if k + 2 < B:
                        stats(m0 + 2, m0 + 2, 0)
                    unit(k + 1, m0 + 1, 1)
                    if k + 2 < B:
                        stats(m0 + 3, m0 + 3, 1)
                    stack_hi2(m0 + 1, 1)
                    transposed(k + 1, m0, k, b, 0)
                    if k + 2 < B:
                        normalise(m0 + 2, m0 + 2, 0)
                if not nxt:
                    ffn_dve(e, 1, 0)
                wo_out(k, b, ("wo", 0), b * 2)
                if k + 2 < B:
                    normalise(m0 + 3, m0 + 3, 1)
                if nxt:
                    transposed(k + 1, m0 + 1, k, b, 1)
                if k + 2 < B:
                    add_norm(m0 + 2, m0 + 2, 0)
                    add_norm(m0 + 3, m0 + 3, 1)
            drive(e, step, B, 1, 3)
            o_norm(B * 2 - 1)
            wo_out(B, B, ("wo", 1), B * 2 - 1)

        def by_heat(e, att):
            hot = e.value_load(hotflag[0:1, 0:1], min_val=0, max_val=1)
            with e.If(hot > 0):
                att(e, True)
            with e.Else():
                att(e, False)

        on_all = [[0, P], [1, 1]]

        @block.sync
        def _(e):
            e.dma_start(X[:, 0:TPC, :], xt[:, 0:TPC, :]).then_inc(s_xin[0], 16)
            e.dma_start(w_int[:, 0:NJ, :], w_gate.rearrange("(j p) d -> p j d", p=P)).then_inc(s_w, 16)
            e.dma_start(w_int[:, NJ:2 * NJ, :], w_up.rearrange("(j p) d -> p j d", p=P))\
                .then_inc(s_w, 16)
            e.dma_start(w_int[:, 2 * NJ:3 * NJ, :], w_down.rearrange("d (j p) -> d j p", p=P))\
                .then_inc(s_w, 16)
            e.dma_start(X[:, TPC:2 * TPC, :], xt[:, TPC:2 * TPC, :]).then_inc(s_xin[1], 16)
            for c in range(2, NC):
                e.wait_ge(s_xin[c % 2], (c // 2) * 16)
                e.dma_start(X[:, c * TPC:(c + 1) * TPC, :], xt[:, c * TPC:(c + 1) * TPC, :])\
                    .then_inc(s_xin[c % 2], 16)
            for c in range(NC):
                e.wait_ge(s_res, NC + c + 1)
                e.dma_start(ot[:, c * TPC:(c + 1) * TPC, :], X[:, c * TPC:(c + 1) * TPC, :])\
                    .then_inc(s_out, 16)
            e.wait_ge(s_out, NC * 16)

        @block.gpsimd
        def _(e):
            e.memset(ident16[:, :], 0.0)
            e.memset(ident32[:, :], 0.0)
            e.memset(causal[:, :], 0.0)
            e.memset(ones32[:, :], 1.0)
            e.memset(nhalf[:, :], -0.5)
            e.memset(eps_ln[:, :], LN_EPS)
            e.memset(eps_rms[:, :], RMS_EPS)
            e.memset(one[:, :], 1.0)
            e.memset(ST[0][:, :, :, 3, :], 0.0)
            e.memset(ST[1][:, :, :, 3, :], 0.0).then_inc(s_const, 1)
            e.wait_ge(s_const, 1)
            e.memset(ST[0][:, :, NH:NQK, 3, 0:2], 1.0)
            e.memset(ST[1][:, :, NH:NQK, 3, 0:2], 1.0)
            for m in (ident16, ident32):
                e.affine_select(out=m[:, :], in_=m[:, :], compare_op=ALU.not_equal, fill=1.0, base=0,
                                pattern=[[-1, P]], channel_multiplier=1)
            e.affine_select(out=causal[:, :], in_=causal[:, :], compare_op=ALU.is_ge, fill=MASKED,
                            base=0, pattern=[[1, P]], channel_multiplier=-1).then_inc(s_const, 1)
            ffn_pool(e, 0, 0)
            ffn_pool(e, 0, 1, {NC - 3: lambda: att_pool(e, ("rstds", 0)),
                               NC - 2: lambda: att_pool(e, ("rstds", 1)),
                               NC - 1: lambda: [att_pool(e, ("x_lo", h)) for h in range(2)]})
            att_pool(e)
            ffn_pool(e, 1, 1)

        @block.scalar
        def _(e):
            e.dma_start(qkvo[:, 0:DQ], wq).then_inc(s_wo_in, 16)
            e.dma_start(qkvo[:, DQ:DQ + DK], wk).then_inc(s_wo_in, 16)
            e.dma_start(qkvo[:, DQ + DK:NQKV], wv).then_inc(s_wo_in, 16)
            e.dma_start(qkvo[:, NQKV:], wo).then_inc(s_wo_in, 16)
            e.dma_start(normw[:, :], norm_w.rearrange("(p a) -> p a", a=1)).then_inc(s_wo_in, 16)
            e.dma_start(gate_t[:, :], bass.AP(gate.tensor, 0, on_all)).then_inc(s_wo_in, 16)
            e.dma_start(lt_t[:, :], bass.AP(log_temp.tensor, 0, on_all)).then_inc(s_wo_in, 16)
            e.wait_ge(s_wo_in, 7 * 16)
            e.activation(k_exp[:, :], lt_t[:, :], ACT.Exp).then_inc(s_kact, 1)
            ffn_act(e, 0, 0)
            w16 = WT[:, :, :, :].rearrange("p s j n -> p (s j) n")
            for r in range(3):
                e.wait_ge(s_wpe, 3 + r)
                lo, hi = 8 * r, min(8 * r + 8, 6 * NJ)
                src = w_bank[r].bitcast(f16).rearrange("p (j n) -> p j n", n=P)
                e.activation(w16[:, lo:hi, :], src[:, 0:hi - lo, :], ACT.Copy).then_inc(s_wt, 1)
            e.wait_ge(s_wready, 1)
            ffn_act(e, 0, 1, {NC - 1: lambda: [att_act(e, False, ("x_hi", h)) for h in range(2)]})
            e.wait_ge(s_wready, 2)
            by_heat(e, att_act)
            ffn_act(e, 1, 1)

        @block.vector
        def _(e):
            n = [0]

            def link(i):
                n[0] += 1
                i.then_inc(s_one, 1)
                e.wait_ge(s_one, n[0])

            ffn_dve(e, 0, 0)
            e.wait_ge(s_w, 3 * 16)
            link(e.tensor_copy(w_flt[:, :, :], w_int[:, :, :]))
            e.tensor_reduce(colmax[:, 0:1], w_flt[:, 0:2 * NJ, :].rearrange("p a b -> p (a b)"), AXX,
                            ALU.max, apply_absolute_value=True)
            e.tensor_reduce(colmax[:, 1:2], w_flt[:, 2 * NJ:, :].rearrange("p a b -> p (a b)"), AXX,
                            ALU.max, apply_absolute_value=True)
            e.wait_ge(s_wo_in, 7 * 16)
            link(e.tensor_scalar(qkvo[:, 0:NQKV], qkvo[:, 0:NQKV], normw[:, 0:1], None, ALU.mult))
            e.tensor_reduce(colmax[:, 2:3], qkvo[:, 0:NQKV], AXX, ALU.max, apply_absolute_value=True)
            e.tensor_reduce(colmax[:, 3:4], qkvo[:, NQKV:], AXX, ALU.max, apply_absolute_value=True)\
                .then_inc(s_wprep, 1)
            e.wait_ge(s_wpe, 1)
            link(e.tensor_reduce(m4[:, 0:1], bank[0][0:4, 0, 0:P], AXX, ALU.max))
            link(e.tensor_scalar(m4[:, 1:2], m4[:, 0:1], 1e-30, None, ALU.max))
            link(e.tensor_scalar(m4[:, 2:3].bitcast(i32), m4[:, 1:2].bitcast(i32), 0x7f800000, None,
                                 ALU.bitwise_and))
            e.tensor_scalar(m4[:, 3:4], m4[:, 2:3], 2.0, None, ALU.mult).then_inc(s_wprep, 1)
            ffn_dve(e, 0, 0.5)
            e.wait_ge(s_wpe, 2)
            link(e.tensor_copy(pw[:, :], bank[1][:, 0, 0:4]))
            link(e.tensor_scalar(ipw[:, :].bitcast(i32), pw[:, :].bitcast(i32), -1.0,
                                 float(0x7f000000), ALU.mult, ALU.add))
            link(e.tensor_scalar(w_flt[:, 0:2 * NJ, :], w_flt[:, 0:2 * NJ, :], ipw[:, 0:1], None,
                                 ALU.mult))
            link(e.tensor_scalar(w_flt[:, 2 * NJ:, :], w_flt[:, 2 * NJ:, :], ipw[:, 1:2], None,
                                 ALU.mult))
            link(e.tensor_copy(w_nat[:, 0, :, :], w_flt[:, :, :]))
            e.tensor_tensor(w_nat[:, 1, :, :], w_flt[:, :, :], w_nat[:, 0, :, :], ALU.subtract)\
                .then_inc(s_wprep, 1)
            e.wait_ge(s_wprep, 3)
            e.tensor_reduce(lomax[:, :], w_nat[:, 1, :, :].rearrange("p a b -> p (a b)"), AXX,
                            ALU.max, apply_absolute_value=True).then_inc(s_wprep, 1)
            link(e.tensor_scalar(k_silu[:, :], pw[:, 0:1], 1.0 / 127.0, None, ALU.mult))
            link(e.reciprocal(k_isilu[:, :], k_silu[:, :]))
            link(e.tensor_scalar(k_ffn[:, :], k_silu[:, :], k_silu[:, 0:1], 0.5 / 127.0, ALU.mult,
                                 ALU.mult))
            link(e.tensor_scalar(k_ffn[:, :], k_ffn[:, :], pw[:, 1:2], None, ALU.mult))
            e.wait_ge(s_wpe, 6)
            link(e.tensor_reduce(lo1[:, :], bank[1][0:1, 1, 0:P], AXX, ALU.max))
            e.tensor_scalar(loflag[:, :], lo1[:, :], 0.0, None, ALU.is_gt).then_inc(s_wready, 1)

            def attention_weights():
                link(e.tensor_scalar(qkvo[:, 0:NQKV], qkvo[:, 0:NQKV], ipw[:, 2:3], None, ALU.mult))
                link(e.tensor_scalar(qkvo[:, NQKV:], qkvo[:, NQKV:], ipw[:, 3:4], None, ALU.mult))
                link(e.tensor_copy(QKVO[:, 0, :], qkvo[:, :]))
                link(e.tensor_tensor(QKVO[:, 1, :], qkvo[:, :], QKVO[:, 0, :], ALU.subtract))
                link(e.tensor_scalar(k_lim[:, :], ipw[:, 2:3], ipw[:, 2:3], None, ALU.mult))
                link(e.tensor_scalar(k_lim[:, :], k_lim[:, :], (L2_MIN / QSCALE) ** 2, 1e-37, ALU.mult,
                                     ALU.max))
                link(e.tensor_scalar(k_wo[:, :], gate_t[:, :], pw[:, 2:3], pw[:, 3:4], ALU.mult, ALU.mult))
                e.wait_ge(s_kact, 1)
                link(e.tensor_scalar(hotflag[:, :], k_exp[0:1, 0:1], HOT, None, ALU.is_gt))
                e.tensor_scalar(k_exp[:, :], k_exp[:, :], 1.0 / (QSCALE * QSCALE), None, ALU.mult)\
                    .then_inc(s_wready, 1)

            def first_rows(stage):
                for half in range(2):
                    att_dve(e, False, (stage, half))
            ffn_dve(e, 0, 1, {NC - 4: lambda: first_rows("stats"),
                              NC - 1: lambda: (first_rows("normalise"), attention_weights()),
                              NC: lambda: first_rows("add_norm")})
            by_heat(e, att_dve)
            ffn_dve(e, 1, 1)

        @block.tensor
        def _(e):
            e.wait_ge(s_const, 2)
            e.wait_ge(s_wprep, 1)
            e.matmul(bank[0][0:4, 0, 0:P], colmax[:, :], ident32[:, :], is_transpose=True,
                     start=True, stop=True).then_inc(s_wpe, 1)
            e.wait_ge(s_wprep, 2)
            e.matmul(bank[1][:, 0, 0:4], m4[:, 3:4].to_broadcast([4, P]), ident32[0:4, 0:4],
                     start=True, stop=True).then_inc(s_wpe, 1)
            e.wait_ge(s_wprep, 3)
            blocks = [(s, j) for s in range(2) for j in range(3 * NJ)]
            for r in range(3):
                dst = w_bank[r].bitcast(f16)
                for a, (s, j) in enumerate(blocks[8 * r:8 * r + 8]):
                    i = e.transpose(dst[:, a * P:(a + 1) * P], w_nat[:, s, j, :], ident16[:, :])
                i.then_inc(s_wpe, 1)
            e.wait_ge(s_wprep, 4)
            e.matmul(bank[1][0:1, 1, 0:P], lomax[:, :], ident32[:, :], is_transpose=True,
                     start=True, stop=True).then_inc(s_wpe, 1)
            ffn_pe(e, 0, 0, 0)
            e.wait_ge(s_wt, 3)
            e.wait_ge(s_wready, 1)
            low = e.value_load(loflag[0:1, 0:1], min_val=0, max_val=1)

            def ffn(ph):
                with e.If(low > 0):
                    ffn_pe(e, ph, 1)
                with e.Else():
                    ffn_pe(e, ph, 0)
            ffn(0)
            e.wait_ge(s_res, NC)
            e.wait_ge(s_wready, 2)
            by_heat(e, att_pe)
            ffn_pe(e, 1, 0, 0)
            ffn(1)


_INS = ["L0_attn_x", "L0_attn_norm_w", "L0_attn_Wq", "L0_attn_Wk", "L0_attn_Wv", "L0_attn_Wo",
        "L0_attn_gate", "L0_attn_log_temperature", "L0_ffn_w_gate", "L0_ffn_w_up", "L0_ffn_w_down"]


def kernel(**inputs):
    import numpy as _np
    import concourse.bacc as _bacc
    from concourse.bass_utils import run_bass_kernel_spmd as _run

    nc = _bacc.Bacc("TRN2", target_bir_lowering=False, num_devices=1)
    arrays, args = {}, []
    for name in _INS:
        a = _np.ascontiguousarray(inputs[name])
        if a.ndim == 0:
            a = a.reshape(1)
        arrays[f"in_{name}"] = a
        args.append(nc.dram_tensor(f"in_{name}", a.shape, mybir.dt.from_np(a.dtype),
                                   kind="ExternalInput").ap())
    shape = arrays["in_L0_attn_x"].shape
    args.append(nc.dram_tensor("result", shape, mybir.dt.float32, kind="ExternalOutput").ap())
    macaron_kernel(nc, *args)
    r = _run(nc, [arrays], core_ids=[0])
    return r.results[0]["result"]
```
